# Optimizing a Trainium2 kernel written in Bass

```python
import numpy as np
import jax
import jax.numpy as jnp

def _softmax(x, axis=-1):
    return jax.nn.softmax(x, axis=axis)
def _gelu(x):
    return jax.nn.gelu(x, approximate=True)
def _silu(x):
    return jax.nn.silu(x)
def _sigmoid(x):
    return jax.nn.sigmoid(x)
def _layernorm(x, axis=-1, eps=1e-5):
    m = jnp.mean(x, axis=axis, keepdims=True)
    v = jnp.var(x, axis=axis, keepdims=True)
    return (x - m) / jnp.sqrt(v + eps)
def _scatter_add(tgt, idx, src, axis=0):
    return tgt.at[idx].add(src)
def _segment_sum(src, seg, n):
    return jax.ops.segment_sum(src, seg, n)

kernel_name = 'mk_adj_preln_d4_adj_128_d39bb3'

def setup_inputs(seed: int = 0):
    np.random.seed(seed)
    _w = jnp.asarray
    def _rec_inputs():
        import jax
        import jax.numpy as jnp
        _gk = jax.random.key(seed)
        x = -0.000929 + 1 * jax.random.normal(jax.random.fold_in(_gk, 1), (8192, 128), jnp.float32)
        _a = jax.random.bernoulli(jax.random.fold_in(_gk, 2), 0.000976562, (8192, 8192))
        _a = jnp.logical_or(_a, jnp.eye(8192, dtype=bool))
        _af = _a.astype(jnp.float32)
        _af = _af * jax.random.uniform(jax.random.fold_in(_gk, 3), (8192, 8192), jnp.float32, 0.05, 1)
        adj = _af
        return x, adj
    x, adj = _rec_inputs()
    def _L0_gnn_setup():
        import jax, jax.numpy as jnp
        import numpy as np
        N = 8192
        H = 128
        key = jax.random.key(seed)
        k_x, k_A, k_W = jax.random.split(key, 3)
        x = jax.random.normal(k_x, (N, H), dtype=jnp.float32)
        A = jax.random.uniform(k_A, (N, N), dtype=jnp.float32)
        alpha = jnp.array([0.5], dtype=jnp.float32)
        bound = 1.0 / np.sqrt(H)
        W = jax.random.uniform(k_W, (H, H), dtype=jnp.float32, minval=-bound, maxval=bound)
        b = jnp.zeros((H,), dtype=jnp.float32)
        t = jnp.zeros((1,), dtype=jnp.float32)
        return {'t': t, 'x': x, 'A': A, 'alpha': alpha, 'W': W, 'b': b}
    _L0_gnn_all = _L0_gnn_setup()
    _L0_gnn_in = {k: v for k, v in _L0_gnn_all.items() if k in ('t', 'alpha', 'W', 'b', )}
    del _L0_gnn_all

    def _L1_gnn_setup():
        import jax, jax.numpy as jnp
        import numpy as np
        EPS = 1e-05
        MIN_NORM = 1e-15

        def _norm(x):
            return jnp.maximum(jnp.linalg.norm(x, axis=-1, keepdims=True), MIN_NORM)

        def _artanh(x):
            return jnp.arctanh(jnp.clip(x, -1.0 + EPS, 1.0 - EPS))

        def expmap0(u):
            un = _norm(u)
            return jnp.tanh(un) * u / un

        def logmap0(y):
            yn = _norm(y)
            return _artanh(yn) * y / yn

        def mobius_matvec(W, x):
            mx = x @ W
            xn = _norm(x)
            mxn = _norm(mx)
            res = jnp.tanh(mxn / xn * _artanh(xn)) * mx / mxn
            zero = jnp.all(mx == 0.0, axis=-1, keepdims=True)
            return jnp.where(zero, 0.0, res)

        def mobius_scalar_mul(r, x):
            xn = _norm(x)
            return jnp.tanh(r * _artanh(xn)) * x / xn

        def _clamp_abs(x, eps=1e-10):
            return jnp.where(x >= 0.0, jnp.maximum(x, eps), jnp.minimum(x, -eps))
        key = jax.random.key(seed)
        k1, k2, k3 = jax.random.split(key, 3)
        N, D_IN, D_OUT = (8192, 128, 128)
        AVG_DEG = 64.0
        v = 0.1 * jax.random.normal(k1, (N, D_IN), dtype=jnp.float32)
        X = expmap0(v)
        mask = (jax.random.uniform(k2, (N, N)) < AVG_DEG / N).astype(jnp.float32)
        mask = mask + jnp.eye(N, dtype=jnp.float32)
        A_hat = mask / mask.sum(-1, keepdims=True)
        W = jax.random.uniform(k3, (D_IN, D_OUT), dtype=jnp.float32)
        return {'X': X, 'A_hat': A_hat, 'W': W}
    _L1_gnn_all = _L1_gnn_setup()
    _L1_gnn_in = {k: v for k, v in _L1_gnn_all.items() if k in ('W', )}
    del _L1_gnn_all

    def _L2_gnn_setup():
        import jax, jax.numpy as jnp
        import numpy as np
        N = 16384
        IN_F = 128
        OUT_F = 128
        TOP_K = 32
        key = jax.random.key(seed)
        kx, ka, kw, kb = jax.random.split(key, 4)
        x = jax.random.normal(kx, (N, IN_F), dtype=jnp.float32)
        adj = jax.random.uniform(ka, (N, N), dtype=jnp.float32)
        W = jax.random.normal(kw, (OUT_F, IN_F), dtype=jnp.float32) * (1.0 / np.sqrt(IN_F))
        b = jax.random.normal(kb, (OUT_F,), dtype=jnp.float32) * 0.01
        return {'x': x, 'adj': adj, 'W': W, 'b': b, 'top_k': TOP_K}
    _L2_gnn_all = _L2_gnn_setup()
    _L2_gnn_in = {k: v for k, v in _L2_gnn_all.items() if k in ('W', 'b', )}
    del _L2_gnn_all

    def _L3_gnn_setup():
        import jax, jax.numpy as jnp
        import numpy as np
        N = 8192
        DIN = 128
        DOUT = 128
        EPS = 1e-07
        GAMMA_MAX = 10000000.0

        def _mobius_scalar_mul(r, x):
            n = jnp.linalg.norm(x, axis=-1, keepdims=True)
            n_safe = jnp.clip(n, EPS, 1.0 - EPS)
            return jnp.tanh(r * jnp.arctanh(n_safe)) * x / n_safe

        def _logmap0(x):
            n = jnp.linalg.norm(x, axis=-1, keepdims=True)
            n_safe = jnp.clip(n, EPS, 1.0 - EPS)
            return jnp.arctanh(n_safe) * x / n_safe

        def _expmap0(v):
            n = jnp.linalg.norm(v, axis=-1, keepdims=True)
            n_safe = jnp.maximum(n, EPS)
            return jnp.tanh(n_safe) * v / n_safe
        key = jax.random.key(seed)
        k1, k2, k3, k4 = jax.random.split(key, 4)
        x = 0.01 * jax.random.normal(k1, (N, DIN), dtype=jnp.float32)
        adj = (jax.random.uniform(k2, (N, N)) < 0.004).astype(jnp.float32)
        W = 0.05 * jax.random.normal(k3, (DIN, DOUT), dtype=jnp.float32)
        b = 0.05 * jax.random.normal(k4, (DOUT,), dtype=jnp.float32)
        return {'x': x, 'adj': adj, 'W': W, 'b': b}
    _L3_gnn_all = _L3_gnn_setup()
    _L3_gnn_in = {k: v for k, v in _L3_gnn_all.items() if k in ('W', 'b', )}
    del _L3_gnn_all

    return {
        "x": x,
        "adj": adj,
        "L0_gnn_t": _L0_gnn_in["t"],
        "L0_gnn_alpha": _L0_gnn_in["alpha"],
        "L0_gnn_W": _L0_gnn_in["W"],
        "L0_gnn_b": _L0_gnn_in["b"],
        "L1_gnn_W": _L1_gnn_in["W"],
        "L2_gnn_W": _L2_gnn_in["W"],
        "L2_gnn_b": _L2_gnn_in["b"],
        "L3_gnn_W": _L3_gnn_in["W"],
        "L3_gnn_b": _L3_gnn_in["b"],
    }

def reference(x, adj, L0_gnn_t, L0_gnn_alpha, L0_gnn_W, L0_gnn_b, L1_gnn_W, L2_gnn_W, L2_gnn_b, L3_gnn_W, L3_gnn_b):
    import jax
    import jax.numpy as jnp
    def _L0_gnn_ref(t, x, A, alpha, W, b):
        import jax, jax.numpy as jnp
        import numpy as np
        N = 8192
        H = 128
        a = alpha[0]
        A_prime = a * A
        diag = jnp.diagonal(A_prime) + (1.0 - a)
        A_prime = A_prime.at[jnp.arange(N), jnp.arange(N)].set(diag)
        out_degree = A_prime.sum(axis=1)
        inv_deg = jnp.where(out_degree == 0.0, 0.0, 1.0 / out_degree)
        x = inv_deg[:, None] * A_prime @ x
        x = x @ W.T + b
        return jax.nn.relu(x)

    def _L1_gnn_ref(X, A_hat, W):
        import jax, jax.numpy as jnp
        import numpy as np
        EPS = 1e-05
        MIN_NORM = 1e-15

        def _norm(x):
            return jnp.maximum(jnp.linalg.norm(x, axis=-1, keepdims=True), MIN_NORM)

        def _artanh(x):
            return jnp.arctanh(jnp.clip(x, -1.0 + EPS, 1.0 - EPS))

        def expmap0(u):
            un = _norm(u)
            return jnp.tanh(un) * u / un

        def logmap0(y):
            yn = _norm(y)
            return _artanh(yn) * y / yn

        def mobius_matvec(W, x):
            mx = x @ W
            xn = _norm(x)
            mxn = _norm(mx)
            res = jnp.tanh(mxn / xn * _artanh(xn)) * mx / mxn
            zero = jnp.all(mx == 0.0, axis=-1, keepdims=True)
            return jnp.where(zero, 0.0, res)

        def mobius_scalar_mul(r, x):
            xn = _norm(x)
            return jnp.tanh(r * _artanh(xn)) * x / xn

        def _clamp_abs(x, eps=1e-10):
            return jnp.where(x >= 0.0, jnp.maximum(x, eps), jnp.minimum(x, -eps))
        XW = mobius_matvec(W, X)
        sq = jnp.sum(XW * XW, axis=-1, keepdims=True)
        gamma = 2.0 / jnp.maximum(1.0 - sq, EPS)
        nominator = A_hat @ (gamma * XW)
        denominator = _clamp_abs(A_hat @ (gamma - 1.0))
        two_mean = nominator / denominator
        m = mobius_scalar_mul(0.5, two_mean)
        r = A_hat.sum(-1, keepdims=True)
        AXW = mobius_scalar_mul(r, m)
        return expmap0(jax.nn.relu(logmap0(AXW)))

    def _L2_gnn_ref(x, adj, W, b, top_k):
        import jax, jax.numpy as jnp
        import numpy as np
        N = 16384
        IN_F = 128
        OUT_F = 128
        TOP_K = 32
        h = jnp.einsum('ni,oi->no', x, W) + b
        _, topk_idx = jax.lax.top_k(adj, top_k)
        h_agg = jnp.max(h[topk_idx], axis=1)
        return h_agg

    def _L3_gnn_ref(x, adj, W, b):
        import jax, jax.numpy as jnp
        import numpy as np
        N = 8192
        DIN = 128
        DOUT = 128
        EPS = 1e-07
        GAMMA_MAX = 10000000.0

        def _mobius_scalar_mul(r, x):
            n = jnp.linalg.norm(x, axis=-1, keepdims=True)
            n_safe = jnp.clip(n, EPS, 1.0 - EPS)
            return jnp.tanh(r * jnp.arctanh(n_safe)) * x / n_safe

        def _logmap0(x):
            n = jnp.linalg.norm(x, axis=-1, keepdims=True)
            n_safe = jnp.clip(n, EPS, 1.0 - EPS)
            return jnp.arctanh(n_safe) * x / n_safe

        def _expmap0(v):
            n = jnp.linalg.norm(v, axis=-1, keepdims=True)
            n_safe = jnp.maximum(n, EPS)
            return jnp.tanh(n_safe) * v / n_safe
        n = adj.shape[0]
        a = jnp.eye(n, dtype=adj.dtype) + adj
        D = 1.0 / jnp.sqrt(jnp.sum(a, axis=1))
        a = a * D[:, None] * D[None, :]
        r2 = jnp.sum(x * x, axis=-1, keepdims=True)
        gamma = jnp.minimum(2.0 / (1.0 - r2), GAMMA_MAX)
        num = a * gamma
        den = jnp.sum(a * (gamma - 1.0), axis=-1, keepdims=True)
        coef = num / den
        aggr = coef @ x
        aggr = _mobius_scalar_mul(0.5, aggr)
        u = _logmap0(aggr)
        y = jax.nn.relu(u @ W + b)
        return _expmap0(y)

    h = jnp.maximum(_layernorm(x, axis=-1), 0.0)
    x = x + _L0_gnn_ref(L0_gnn_t, h, adj, L0_gnn_alpha, L0_gnn_W, L0_gnn_b)
    h = jnp.maximum(_layernorm(x, axis=-1), 0.0)
    x = x + _L1_gnn_ref(h, adj, L1_gnn_W)
    h = jnp.maximum(_layernorm(x, axis=-1), 0.0)
    x = x + _L2_gnn_ref(h, adj, L2_gnn_W, L2_gnn_b, 32)
    h = jnp.maximum(_layernorm(x, axis=-1), 0.0)
    x = x + _L3_gnn_ref(h, adj, L3_gnn_W, L3_gnn_b)
    return x


_drawn_inputs = setup_inputs


def setup_inputs(seed=0):
    import zlib

    import numpy as np

    out = dict(_drawn_inputs(seed))
    spreads = {'L0_gnn_b': (0.0, 0.1)}
    factors = {'L1_gnn_W': 64.0, 'L2_gnn_b': 8.0, 'L3_gnn_W': 57.505, 'L3_gnn_b': 3.605}
    for name, (base, spread) in spreads.items():
        noise = np.random.default_rng([zlib.crc32(name.encode()), seed]).standard_normal(out[name].shape)
        drawn = base * np.exp(spread * noise) if base else spread * noise
        out[name] = jnp.asarray(drawn.astype(out[name].dtype))
    for name, factor in factors.items():
        out[name] = (out[name] * factor).astype(out[name].dtype)
    return out
```

```python
import concourse.bass as bass
from concourse import mybir
from contextlib import ExitStack

P = 128
TPG = 4
GROUP = TPG * P
PIECE = 512
SLOTS = 4
TOPK = 32
PREFIX = 64
NGATHER = TOPK + 1
COMMON = 14
CUTS = [16, 17, 18, 19, 20, 22, 25, NGATHER]
ROUNDS = TOPK // 8
LN_EPS = 1e-5

fp32 = mybir.dt.float32
u32 = mybir.dt.uint32
i32 = mybir.dt.int32
ALU = mybir.AluOpType
ACT = mybir.ActivationFunctionType
AX = mybir.AxisListType
RMAX = bass.bass_isa.ReduceOp.max


class Steps:

    def __init__(self, engine, semaphore, carrier):
        self.engine, self.semaphore, self.carrier = engine, semaphore, carrier
        self.base, self.turn, self.per, self.k = 0, None, 0, 0

    def value(self, k):
        return self.base + k if self.turn is None else self.turn * self.per + (self.base + k)

    def mark(self, instruction):
        instruction.then_inc(self.semaphore, 1)
        self.k += 1
        return self.k

    def settle(self, k=None, tell=None):
        self.engine.wait_ge(self.semaphore, self.value(self.k if k is None else k))
        if tell is not None:
            self.engine.sem_inc(tell, 1)
        elif self.turn is not None:
            self.engine.sem_inc(self.carrier, 1)

    def link(self, instruction, tell=None):
        self.mark(instruction)
        self.settle(tell=tell)

    def enter(self, turn, per):
        self.base, self.turn, self.per, self.k = self.base + self.k, turn, per, 0

    def leave(self, turns):
        assert self.k == self.per, (self.k, self.per)
        self.base, self.turn, self.k = self.base + turns * self.per, None, 0


def build(nc, x, adj, alpha, w0, b0, w1, w2, b2, w3, b3, out):
    N = x.shape[0]
    NT = N // P
    NG = NT // TPG
    NPC = N // PIECE
    BPP = PIECE // P
    NP = NT // 2
    K4 = NPC // SLOTS
    assert NG % 2 == 0 and NPC % SLOTS == 0

    x_v = x.rearrange("(t p) f -> p t f", p=P)
    out_v = out.rearrange("(t p) f -> p t f", p=P)
    adj_v = adj.rearrange("(g r p) (c x) -> g c p r x", p=P, r=TPG, x=PIECE)
    adj_rows = adj.rearrange("(t p) n -> t p n", p=P)
    table = nc.dram_tensor("h_table", (N + PREFIX, P), fp32).ap()
    dot_d = nc.dram_tensor("dot_row", (NT, P), fp32).ap()

    ctx = ExitStack()
    with ctx:
        def sb(name, shape, dt=fp32):
            return ctx.enter_context(nc.sbuf_tensor(name, shape, dt))

        def pb(name, shape):
            return ctx.enter_context(nc.psum_tensor(name, shape, fp32))

        def sem(name):
            return ctx.enter_context(nc.semaphore(name))

        X = sb("X", [P, NT, P])
        H = sb("H", [P, NT, P])
        AGG = sb("AGG", [P, NT, P])
        D = sb("D", [P, max(N, NGATHER * P)])
        PIECES = sb("PIECES", [P, max(SLOTS * TPG * PIECE, NGATHER * P, N)])
        AT = [sb(f"AT{i}", [P, 2 * GROUP]) for i in range(2)]
        aggT = sb("aggT", [P, GROUP])
        gmax = sb("gmax", [P, P])
        ident = sb("ident", [P, P])
        wnat = sb("wnat", [P, 2, P])
        W = [sb(f"W{i}", [P, P]) for i in range(4)]
        bias = sb("bias", [P, 3, P])
        alph = sb("alph", [P, 2])
        IDX = sb("IDX", [P, NT + 2, NGATHER], mybir.dt.uint16)
        idx_now = [sb(f"idx_now{i}", [P, NGATHER], u32) for i in range(2)]
        rs_part = sb("rs_part", [P, TPG, NPC])
        dp_part = sb("dp_part", [P, TPG, NPC])
        RS = sb("RS", [P, NT])
        DEN = sb("DEN", [P, NT])
        FLAGS = sb("FLAGS", [P, 2, NT])
        FLAGR = sb("FLAGR", [P, 2, NT])
        CTL = sb("CTL", [1, 3, NT], i32)
        ctlf = sb("ctlf", [1, 2, NT])
        sm = sb("sm", [P, 14, NT])
        dots = sb("dots", [P, NT])
        drow = sb("drow", [NT, P])
        s4 = sb("s4", [P, 10, TPG])
        f8 = sb("f8", [P, 8])
        fidx = sb("fidx", [P, TOPK], u32)
        pfx = sb("pfx", [P, 2, PREFIX])
        pfxn = sb("pfxn", [PREFIX, P])

        pieces = [PIECES[:, i * TPG * PIECE:(i + 1) * TPG * PIECE].rearrange("p (r x) -> p r x", r=TPG)
                  for i in range(SLOTS)]
        SQ = D[:, 0:N].rearrange("p (t f) -> p t f", f=P)
        ring = [B[:, 0:NGATHER * P].rearrange("p (k f) -> p k f", f=P) for B in (D, PIECES)]
        CW = NPC * 8
        at = [0]

        def part(n):
            at[0] += n
            assert at[0] <= D.shape[1]
            return D[:, at[0] - n:at[0]]

        cand = part(TPG * CW).rearrange("p (r c e) -> p r c e", r=TPG, e=8)
        cidx = part(TPG * CW).bitcast(u32).rearrange("p (r c e) -> p r c e", r=TPG, e=8)
        cbase = part(TPG * CW).rearrange("p (r c e) -> p r c e", r=TPG, e=8)
        pos = part(TPG * CW).rearrange("p (r c e) -> p r c e", r=TPG, e=8)
        keys = part(TPG * CW).rearrange("p (r k) -> p r k", r=TPG)
        zero = part(TPG * PREFIX).rearrange("p (r k) -> p r k", r=TPG)
        zcum = part(TPG * PREFIX).rearrange("p (r k) -> p r k", r=TPG)
        ones = part(PREFIX)
        top = part(TPG * TOPK).rearrange("p (r k) -> p r k", r=TPG)
        topm = part(TPG * TOPK).rearrange("p (r k) -> p r k", r=TPG)
        topd = part(TPG * TOPK).rearrange("p (r k) -> p r k", r=TPG)

        psT = [pb(f"psT{i}", [P, 2 * GROUP]) for i in range(2)]
        psA = pb("psA", [P, GROUP])
        psN = pb("psN", [P, GROUP])
        psX = pb("psX", [P, GROUP])
        psY = pb("psY", [P, GROUP])
        junk = [psX, psY]

        s_load = sem("s_load")
        s_ident = sem("s_ident")
        ident_ready = sem("ident_ready")
        pick_constants = sem("pick_constants")
        prefix_copied = sem("prefix_copied")
        weights_transposed = sem("weights_transposed")
        carrier = {e: sem(f"carrier_{e}") for e in ("dve", "act", "pe", "sp", "pool")}
        dve_step = sem("dve_step")
        pick_step = sem("pick_step")
        act_step = sem("act_step")
        piece_loaded = [sem(f"piece_loaded{i}") for i in range(SLOTS)]
        pass_ready = sem("pass_ready")
        pass_dots = sem("pass_dots")
        pair_transposed = [sem(f"pair_transposed{q}") for q in range(3)]
        piece_scanned = [sem(f"piece_scanned{q}") for q in range(3)]
        piece_summed = sem("piece_summed")
        pair_copied = sem("pair_copied")
        pair_used = sem("pair_used")
        acc_copied = sem("acc_copied")
        nat_ready = sem("nat_ready")
        nat_copied = sem("nat_copied")
        rs_reduced = sem("rs_reduced")
        flags_ready = sem("flags_ready")
        flags_reduced = sem("flags_reduced")
        ctl_ready = sem("ctl_ready")
        row_loaded = sem("row_loaded")
        row_used = sem("row_used")
        general_step = sem("general_step")
        for_act = sem("for_act")
        from_act = sem("from_act")
        proj_start = sem("proj_start")
        staged = sem("staged")
        stage_read = sem("stage_read")
        hT_copied = sem("hT_copied")
        projected = sem("projected")
        proj_out = sem("proj_out")
        dots_small = sem("dots_small")
        dots_turned = sem("dots_turned")
        drow_copied = sem("drow_copied")
        dots_stored = sem("dots_stored")
        dots_spread = sem("dots_spread")
        h_ready = sem("h_ready")
        prefix_t = sem("prefix_t")
        prefix_scanned = sem("prefix_scanned")
        prefix_n = sem("prefix_n")
        prefix_ready = sem("prefix_ready")
        table_stored = sem("table_stored")
        idx_staged = sem("idx_staged")
        gathered = [sem(f"gathered{i}") for i in range(2)]
        reduced = sem("reduced")
        gather_step = sem("gather_step")
        x_done = sem("x_done")
        s_out = sem("s_out")

        block = ctx.enter_context(nc.Block())
        LOADS = 9 * 16
        PICK = 22 + 2 * ROUNDS * TPG
        SCAN = [2 * TPG, TPG, TPG]
        FULL = 16 * NGATHER

        def tiles_of(A, g):
            return A[:, bass.ds(g * TPG, TPG)]

        @block.sync
        def _(sp):
            sp.dma_start(X[:, :, :], x_v).then_inc(s_load, 16)
            sp.dma_start(wnat[:, 0, :], w0).then_inc(s_load, 16)
            sp.dma_start(wnat[:, 1, :], w2).then_inc(s_load, 16)
            sp.dma_start(W[1][:, :], w1).then_inc(s_load, 16)
            sp.dma_start(W[3][:, :], w3).then_inc(s_load, 16)
            for n, b in enumerate((b0, b2, b3)):
                sp.dma_start(bias[:, n, :], b.partition_broadcast(P)).then_inc(s_load, 16)
            sp.dma_start(alph[:, 0:1], alpha.partition_broadcast(P)).then_inc(s_load, 16)

            def load_pieces(q):
                with sp.Fori(0, NG) as g:
                    for c in range(NPC):
                        sp.wait_ge(pair_transposed[q], g * (2 * NPC) + 2 * (c + 1))
                        sp.sem_inc(carrier["sp"], 1)
                        sp.wait_ge(piece_scanned[q], g * (NPC * SCAN[q]) + SCAN[q] * (c + 1))
                        if q == 0:
                            sp.sem_inc(carrier["sp"], 1)
                            sp.wait_ge(piece_summed, g * NPC + (c + 1))
                        sp.sem_inc(carrier["sp"], 1)
                        sp.dma_start(pieces[c % SLOTS], adj_v[bass.ds(g, 1), c, :, :, :])\
                          .then_inc(piece_loaded[c % SLOTS], 16)

            def spread_dots(n):
                sp.wait_ge(drow_copied, n + 1)
                sp.dma_start(dot_d, drow[:, :]).then_inc(dots_stored, 16)
                sp.wait_ge(dots_stored, 16 * (n + 1))
                sp.dma_start(D[:, 0:N], dot_d.rearrange("(o t) f -> o (t f)", o=1)[0, :].partition_broadcast(P))\
                  .then_inc(dots_spread, 16)

            load_pieces(0)

            sp.wait_ge(ctl_ready, 1)
            any_general = sp.value_load(CTL[0:1, 2, 0:1], min_val=0, max_val=1)
            with sp.If(any_general > 0):
                with sp.Fori(0, NT) as t:
                    general = sp.value_load(CTL[0:1, 1, bass.ds(t, 1)], min_val=0, max_val=1)
                    sp.wait_ge(row_used, t + 1)
                    sp.sem_inc(carrier["sp"], 1)
                    with sp.If(general > 0):
                        sp.dma_start(PIECES[:, 0:N], adj_rows[bass.ds(t, 1), :, :]).then_inc(row_loaded, 16)
                    with sp.Else():
                        sp.dma_start(PIECES[0:16, 0:8], adj_rows[0, 0:16, 0:8]).then_inc(row_loaded, 16)

            spread_dots(0)
            load_pieces(1)

            sp.wait_ge(h_ready, 1)
            sp.dma_start(table[0:N, :].rearrange("(t p) f -> p t f", p=P), AGG[:, :, :]).then_inc(table_stored, 16)
            sp.wait_ge(prefix_ready, 1)
            sp.dma_start(table[N:N + PREFIX, :], pfxn[:, :]).then_inc(table_stored, 16)

            spread_dots(1)
            load_pieces(2)

            sp.wait_ge(x_done, 1)
            sp.dma_start(out_v, X[:, :, :]).then_inc(s_out, 16)
            sp.wait_ge(s_out, 16)
            sp.wait_ge(table_stored, 32)
            sp.wait_ge(dots_stored, 32)

        @block.gpsimd
        def _(pool):
            pool.memset(ident[:, :], 0.0).then_inc(s_ident, 1)
            pool.wait_ge(s_ident, 1)
            pool.affine_select(out=ident[:, :], in_=ident[:, :], compare_op=ALU.not_equal, fill=1.0,
                               base=0, pattern=[[-1, P]], channel_multiplier=1).then_inc(ident_ready, 1)
            pool.memset(IDX[:, NT:NT + 2, :], 0).then_inc(ident_ready, 1)
            pool.wait_ge(pass_ready, 1)
            pool.memset(ones, 1.0).then_inc(pick_constants, 1)
            pool.iota(cbase, [[0, TPG], [PIECE, NPC], [0, 8]], base=1, channel_multiplier=0,
                      allow_small_or_imprecise_dtypes=True).then_inc(pick_constants, 1)

            pool.wait_ge(flags_ready, 1)
            pool.partition_all_reduce(FLAGR[:, :, :].rearrange("p a t -> p (a t)"),
                                      FLAGS[:, :, :].rearrange("p a t -> p (a t)"), P, RMAX)\
                .then_inc(flags_reduced, 1)

            def gather(par, k, inc):
                pool.indirect_dma_start(ring[par][:, k, :], None, table,
                                        bass.IndirectOffsetOnAxis(ap=idx_now[par][:, k:k + 1], axis=0))\
                    .then_inc(gathered[par], inc)

            def gathers(par, n, cuts):
                def leaf(count):
                    for k in range(COMMON, count):
                        share = (NGATHER - COMMON) * (k + 1 - COMMON) // (count - COMMON) - \
                            (NGATHER - COMMON) * (k - COMMON) // (count - COMMON)
                        gather(par, k, 16 * share)
                if len(cuts) == 1:
                    leaf(cuts[0])
                    return
                with pool.If(n < cuts[0] + 1):
                    leaf(cuts[0])
                with pool.Else():
                    gathers(par, n, cuts[1:])

            pool.wait_ge(ctl_ready, 1)
            pool.wait_ge(table_stored, 32)
            with pool.Fori(0, NT // 2) as i:
                for par in range(2):
                    n = pool.value_load(CTL[0:1, 0, bass.ds(i * 2 + par, 1)], min_val=1, max_val=NGATHER)
                    pool.wait_ge(idx_staged, i * 2 + (par + 1))
                    pool.sem_inc(carrier["pool"], 1)
                    for k in range(COMMON):
                        gather(par, k, 16)
                    gathers(par, n, CUTS)

        @block.tensor
        def _(pe):
            pe.wait_ge(s_load, LOADS)
            pe.wait_ge(ident_ready, 2)
            nc.tensor.transpose(psX[:, 0:P], wnat[:, 0, :], ident[:, :])
            nc.tensor.transpose(psX[:, P:2 * P], wnat[:, 1, :], ident[:, :]).then_inc(weights_transposed, 1)

            def project(n, w):
                with pe.Fori(0, NG // 2) as i:
                    for h in range(2):
                        pe.wait_ge(staged, i * 2 + (n * NG + h + 1))
                        for r in range(TPG):
                            last = nc.tensor.transpose(psT[h][:, r * P:(r + 1) * P],
                                                       AT[h][:, r * P:(r + 1) * P], ident[:, :])
                        last.then_inc(stage_read, 1)
                    for h, ps in enumerate((psX, psY)):
                        pe.wait_ge(hT_copied, i * 2 + (n * NG + h + 1))
                        pe.wait_ge(proj_out, i * 2 + (n * NG + h + 1))
                        for r in range(TPG):
                            last = nc.tensor.matmul(ps[:, r * P:(r + 1) * P],
                                                    AT[h][:, GROUP + r * P:GROUP + (r + 1) * P], W[w][:, :],
                                                    start=True, stop=True)
                        last.then_inc(projected, 1)

            def adjacency_pass(q):
                pe.wait_ge(pass_ready, q + 1)
                with pe.Fori(0, NG) as g:
                    def turn_pair(k):
                        if k % 2 == 0:
                            c = k // 2
                            pe.wait_ge(piece_loaded[c % SLOTS], g * (16 * K4) + 16 * (q * NG * K4 + c // SLOTS + 1))
                        pe.wait_ge(pair_copied, g * NP + (q * NG * NP + k + 1))
                        for b in range(2):
                            x0 = (k % 2) * 2 * P + b * P
                            for r in range(TPG):
                                last = nc.tensor.transpose(psT[k % 2][:, b * GROUP + r * P:b * GROUP + (r + 1) * P],
                                                           pieces[(k // 2) % SLOTS][:, r, x0:x0 + P], ident[:, :])
                        last.then_inc(pair_transposed[q], 1)

                    turn_pair(0)
                    for k in range(NP):
                        if k + 1 < NP:
                            turn_pair(k + 1)
                        pe.wait_ge(pair_copied, g * NP + (q * NG * NP + k + 1 + 2))
                        if k == 0:
                            pe.wait_ge(acc_copied, g + (q * NG + 1))
                        for b in range(2):
                            j = 2 * k + b
                            last = nc.tensor.matmul(psA[:, :], H[:, j, :], AT[k % 2][:, b * GROUP:(b + 1) * GROUP],
                                                    start=(j == 0), stop=(j == NT - 1))
                        last.then_inc(pair_used, 1)
                    pe.wait_ge(acc_copied, g + (q * NG + 2))
                    pe.wait_ge(nat_copied, g + (q * NG + 1))
                    for r in range(TPG):
                        last = nc.tensor.transpose(psN[:, r * P:(r + 1) * P], aggT[:, r * P:(r + 1) * P], ident[:, :])
                    last.then_inc(nat_ready, 1)

            def turn_dots(n):
                pe.wait_ge(dots_small, n + 1)
                nc.tensor.transpose(psX[0:NT, 0:P], dots[:, :], ident[:, :]).then_inc(dots_turned, 1)

            pe.sem_inc(pair_transposed[0], 2 * SLOTS)
            pe.sem_inc(pair_used, 2)
            pe.sem_inc(stage_read, 2)
            pe.sem_inc(nat_ready, 1)
            pe.sem_inc(projected, 2)
            project(0, 0)
            adjacency_pass(0)
            pe.sem_inc(pair_transposed[1], 2 * SLOTS)
            project(1, 1)
            turn_dots(0)
            adjacency_pass(1)
            pe.sem_inc(pair_transposed[2], 2 * SLOTS)
            project(2, 2)
            pe.wait_ge(h_ready, 1)
            nc.tensor.transpose(psX[:, 0:PREFIX], AGG[0:PREFIX, 0, :], ident[0:PREFIX, 0:PREFIX]).then_inc(prefix_t, 1)
            pe.wait_ge(prefix_scanned, 1)
            nc.tensor.transpose(psY[0:PREFIX, 0:P], pfx[:, 1, :], ident[:, :]).then_inc(prefix_n, 1)
            turn_dots(1)
            adjacency_pass(2)
            project(3, 3)

        @block.scalar
        def _(act):
            st = Steps(act, act_step, carrier["act"])
            asked = [0]

            def job(out, in_, func, **kw):
                asked[0] += 1
                act.wait_ge(for_act, asked[0])
                nc.scalar.activation(out, in_, func, **kw).then_inc(from_act, 1)

            def project(n, dest):
                with act.Fori(0, NG // 2) as i:
                    for h in range(2):
                        act.wait_ge(stage_read, i * 2 + (n * NG + h + 1 + 2))
                        act.wait_ge(projected, i * 2 + (n * NG + h + 1))
                        act.sem_inc(carrier["act"], 1)
                        nc.scalar.activation(AT[h][:, GROUP:2 * GROUP], psT[h][:, 0:GROUP], ACT.Copy)\
                            .then_inc(hT_copied, 1)
                    for h, ps in enumerate((psX, psY)):
                        act.wait_ge(projected, i * 2 + (n * NG + h + 1 + 2))
                        act.sem_inc(carrier["act"], 1)
                        nc.scalar.activation(tiles_of(dest, i * 2 + h), ps[:, :], ACT.Copy).then_inc(proj_out, 1)

            def adjacency_pass(q):
                with act.Fori(0, NG) as g:
                    if q == 0:
                        st.enter(g, TPG * NPC)
                    for k in range(NP):
                        act.wait_ge(pair_transposed[q], g * NP + (k + 1 + 2 * SLOTS))
                        act.wait_ge(pair_used, g * NP + (q * NG * NP + k + 1))
                        nc.scalar.activation(AT[k % 2][:, :], psT[k % 2][:, :], ACT.Copy).then_inc(pair_copied, 1)
                        if q == 0 and k % 2 == 1:
                            c = k // 2
                            if c == 0:
                                act.wait_ge(rs_reduced, g + 1)
                                act.sem_inc(carrier["act"], 1)
                            act.wait_ge(piece_loaded[c % SLOTS], g * (16 * K4) + 16 * (c // SLOTS + 1))
                            act.sem_inc(carrier["act"], 1)
                            for r in range(TPG):
                                if r >= 2:
                                    st.settle(st.k - 1)
                                st.mark(nc.scalar.activation(junk[r % 2][:, :], pieces[c % SLOTS][:, r, :], ACT.Copy,
                                                             accum_out=rs_part[:, r, c:c + 1]))
                            st.settle(tell=piece_summed)
                    act.wait_ge(pair_used, g * NP + (q * NG * NP + NP + 2))
                    act.wait_ge(nat_ready, g + (q * NG + 1))
                    act.sem_inc(carrier["act"], 1)
                    nc.scalar.activation(aggT[:, :], psA[:, :], ACT.Copy).then_inc(acc_copied, 1)
                    act.wait_ge(nat_ready, g + (q * NG + 2))
                    act.sem_inc(carrier["act"], 1)
                    nc.scalar.activation(tiles_of(AGG, g), psN[:, :], ACT.Copy).then_inc(nat_copied, 1)
                if q == 0:
                    st.leave(NG)

            def artanh():
                job(sm[:, 13, :], sm[:, 12, :], ACT.Ln)

            def layernorm():
                job(SQ, H[:, :, :], ACT.Square)
                job(sm[:, 1, :], sm[:, 0, :], ACT.Sqrt)

            def copy_dots():
                act.wait_ge(dots_turned, copy_dots.n + 1)
                copy_dots.n += 1
                nc.scalar.activation(drow[:, :], psX[0:NT, 0:P], ACT.Copy).then_inc(drow_copied, 1)

            copy_dots.n = 0

            act.sem_inc(piece_summed, SLOTS)
            act.sem_inc(pair_copied, 2)
            act.sem_inc(acc_copied, 1)
            act.sem_inc(nat_copied, 1)
            act.sem_inc(proj_out, 2)
            act.wait_ge(weights_transposed, 1)
            st.mark(nc.scalar.activation(W[0][:, :], psX[:, 0:P], ACT.Copy))
            st.mark(nc.scalar.activation(W[2][:, :], psX[:, P:2 * P], ACT.Copy))
            st.settle()
            layernorm()
            project(0, H)
            adjacency_pass(0)
            job(H[:, :, :], H[:, :, :], ACT.Copy, scale=alph[:, 1:2])
            layernorm()
            job(SQ, H[:, :, :], ACT.Square)
            project(1, AGG)
            job(SQ, AGG[:, :, :], ACT.Square)
            job(sm[:, 2:4, :], sm[:, 2:4, :], ACT.Sqrt)
            artanh()
            job(sm[:, 5, :], sm[:, 5, :], ACT.Tanh)
            copy_dots()
            adjacency_pass(1)
            job(SQ, AGG[:, :, :], ACT.Square)
            job(sm[:, 2, :], sm[:, 2, :], ACT.Sqrt)
            artanh()
            job(sm[:, 4, :], sm[:, 4, :], ACT.Tanh, scale=0.5)
            artanh()
            job(sm[:, 6, :], sm[:, 6, :], ACT.Tanh)
            artanh()
            job(SQ, AGG[:, :, :], ACT.Square)
            job(sm[:, 2, :], sm[:, 2, :], ACT.Sqrt)
            job(sm[:, 3, :], sm[:, 2, :], ACT.Tanh)
            layernorm()
            project(2, AGG)
            act.wait_ge(prefix_t, 1)
            nc.scalar.activation(pfx[:, 0, :], psX[:, 0:PREFIX], ACT.Copy).then_inc(prefix_copied, 1)
            act.wait_ge(prefix_n, 1)
            nc.scalar.activation(pfxn[:, :], psY[0:PREFIX, 0:P], ACT.Copy).then_inc(prefix_ready, 1)
            layernorm()
            job(SQ, H[:, :, :], ACT.Square)
            job(sm[:, 3, :], sm[:, 3, :], ACT.Sqrt)
            copy_dots()
            adjacency_pass(2)
            job(SQ, AGG[:, :, :], ACT.Square)
            job(sm[:, 2, :], sm[:, 2, :], ACT.Sqrt)
            artanh()
            job(sm[:, 4, :], sm[:, 4, :], ACT.Tanh, scale=0.5)
            artanh()
            project(3, AGG)
            job(SQ, AGG[:, :, :], ACT.Square)
            job(sm[:, 2, :], sm[:, 2, :], ACT.Sqrt)
            job(sm[:, 3, :], sm[:, 2, :], ACT.Tanh)

        @block.vector
        def _(dve):
            v = nc.vector
            st = Steps(dve, dve_step, carrier["dve"])
            link, mark, settle = st.link, st.mark, st.settle
            asked = [0]

            def S(k):
                return sm[:, k, :]

            def ask():
                asked[0] += 1
                dve.sem_inc(for_act, 1)
                dve.wait_ge(from_act, asked[0])

            def by_row(a):
                return a.unsqueeze(2).to_broadcast([P, NT, P])

            def by_feature(n):
                return bias[:, n, :].unsqueeze(1).to_broadcast([P, NT, P])

            def layernorm():
                link(v.tensor_reduce(S(0), X[:, :, :], AX.X, ALU.add))
                link(v.tensor_scalar(S(0), S(0), -1.0 / P, None, ALU.mult))
                link(v.tensor_tensor(H[:, :, :], X[:, :, :], by_row(S(0)), ALU.add))
                ask()
                link(v.tensor_reduce(S(0), SQ, AX.X, ALU.add))
                link(v.tensor_scalar(S(0), S(0), 1.0 / P, LN_EPS, ALU.mult, ALU.add))
                ask()
                link(v.reciprocal(S(1), S(1)))
                link(v.scalar_tensor_tensor(H[:, :, :], H[:, :, :], 0.0, by_row(S(1)), ALU.max, ALU.mult))

            def squares(k):
                ask()
                link(v.tensor_reduce(S(k), SQ, AX.X, ALU.add))

            def artanh(out, y):
                a, q, y2, m = S(12), S(11), S(10), S(9)
                link(v.tensor_scalar(q, y, -1.0, 1.0, ALU.mult, ALU.add))
                link(v.reciprocal(q, q))
                link(v.scalar_tensor_tensor(a, y, 1.0, q, ALU.add, ALU.mult))
                ask()
                link(v.tensor_tensor(y2, y, y, ALU.mult))
                link(v.tensor_scalar(q, y2, 1.0 / 13, None, ALU.mult))
                for k in (11, 9, 7, 5, 3):
                    link(v.scalar_tensor_tensor(q, q, 1.0 / k, y2, ALU.add, ALU.mult))
                link(v.scalar_tensor_tensor(q, q, 1.0, y, ALU.add, ALU.mult))
                link(v.tensor_scalar(m, y, 0.25, None, ALU.is_lt))
                link(v.scalar_tensor_tensor(q, S(13), -0.5, q, ALU.mult, ALU.add))
                link(v.tensor_tensor(q, q, m, ALU.mult))
                link(v.scalar_tensor_tensor(out, S(13), 0.5, q, ALU.mult, ALU.add))

            def project(n, src):
                with dve.Fori(0, NG // 2) as i:
                    for h in range(2):
                        dve.wait_ge(stage_read, i * 2 + (n * NG + h + 1))
                        dve.sem_inc(carrier["dve"], 1)
                        v.tensor_copy(AT[h][:, 0:GROUP], tiles_of(src, i * 2 + h)).then_inc(staged, 1)
                dve.wait_ge(proj_out, (n + 1) * NG + 2)

            def pick(g):
                cf = [a.rearrange("p r c e -> p (r c e)") for a in (cand, cidx, cbase, pos)]
                kf = keys.rearrange("p r k -> p (r k)")
                pk.mark(v.tensor_tensor(kf, cf[1], cf[2], ALU.add))
                pk.mark(v.tensor_scalar(cf[3], cf[0], 0.0, None, ALU.is_gt))
                pk.mark(v.tensor_reduce(s4[:, 0, :], cand[:, :, :, 7], AX.X, ALU.max))
                pk.settle()
                pk.mark(v.tensor_tensor(kf, kf, cf[3], ALU.mult))
                pk.mark(v.tensor_reduce(s4[:, 1, :], pos.rearrange("p r c e -> p r (c e)"), AX.X, ALU.add))
                for r in range(TPG):
                    pk.mark(v.tensor_tensor_scan(zcum[:, r, :], ones, zero[:, r, :], 0.0, ALU.mult, ALU.add))
                pk.settle()
                pk.mark(v.tensor_scalar(s4[:, 2, :], s4[:, 1, :], -1.0, float(TOPK), ALU.mult, ALU.add))
                for rd in range(ROUNDS):
                    for r in range(TPG):
                        pk.mark(v.max(top[:, r, rd * 8:rd * 8 + 8], keys[:, r, :]))
                    pk.settle()
                    if rd + 1 < ROUNDS:
                        for r in range(TPG):
                            pk.mark(v.match_replace(keys[:, r, :], top[:, r, rd * 8:rd * 8 + 8], keys[:, r, :], 0.0))
                        pk.settle()
                pk.mark(v.tensor_tensor(zcum, zcum, s4[:, 2, :].unsqueeze(2).to_broadcast([P, TPG, PREFIX]), ALU.is_lt))
                pk.mark(v.tensor_scalar(topm, top, 0.0, None, ALU.is_gt))
                pk.mark(v.tensor_scalar(s4[:, 4, :], s4[:, 0, :], 0.0, None, ALU.is_gt))
                pk.settle()
                pk.mark(v.tensor_reduce(s4[:, 3, :], zcum, AX.X, ALU.add))
                pk.mark(v.scalar_tensor_tensor(s4[:, 4, :], s4[:, 1, :], float(TOPK) - 0.5, s4[:, 4, :], ALU.is_gt, ALU.max))
                pk.mark(v.tensor_scalar(s4[:, 5, :], s4[:, 6, :], 0.0, None, ALU.is_lt))
                pk.settle()
                pk.mark(v.tensor_scalar(s4[:, 3, :], s4[:, 3, :], float(N), None, ALU.add))
                pk.mark(v.tensor_tensor(tiles_of(FLAGS[:, 1, :], g), s4[:, 4, :], s4[:, 5, :], ALU.max))
                pk.mark(v.tensor_copy(tiles_of(FLAGS[:, 0, :], g), s4[:, 1, :]))
                pk.settle()
                slot0 = s4[:, 3, :].unsqueeze(2).to_broadcast([P, TPG, TOPK])
                pk.mark(v.scalar_tensor_tensor(topd, top, -1.0, slot0, ALU.add, ALU.subtract))
                pk.settle()
                pk.mark(v.tensor_tensor(topd, topd, topm, ALU.mult))
                pk.settle()
                pk.mark(v.tensor_tensor(tiles_of(IDX[:, :, 1:NGATHER], g), topd, slot0, ALU.add))
                pk.mark(v.tensor_copy(tiles_of(IDX[:, :, 0], g), s4[:, 3, :]))
                pk.settle()

            def scan_pass():
                with dve.Fori(0, NG) as g:
                    sc.enter(g, SCAN[0] * NPC)
                    pk.enter(g, PICK)
                    for c in range(NPC):
                        dve.wait_ge(piece_loaded[c % SLOTS], g * (16 * K4) + 16 * (c // SLOTS + 1))
                        dve.sem_inc(carrier["dve"], 1)
                        pc = pieces[c % SLOTS]
                        if c == 0:
                            pk.mark(v.tensor_scalar(zero, pc[:, :, 0:PREFIX], 0.0, None, ALU.is_equal))
                            pk.mark(v.tensor_reduce(s4[:, 6, :], pc[:, :, 0:PREFIX], AX.X, ALU.min))
                            pk.settle()
                        found = []
                        for r in range(TPG + 1):
                            if r < TPG:
                                found.append(sc.mark(v.max(cand[:, r, c, :], pc[:, r, :])))
                            if r:
                                sc.settle(found[r - 1])
                                sc.mark(v.max_index(cidx[:, r - 1, c, :], cand[:, r - 1, c, :], pc[:, r - 1, :]))
                    sc.settle()
                    dve.wait_ge(pick_constants, 2)
                    pick(g)
                    dve.wait_ge(piece_summed, g * NPC + (NPC + SLOTS))
                    dve.sem_inc(carrier["dve"], 1)
                    pk.mark(v.tensor_reduce(tiles_of(RS[:, :], g), rs_part[:, :, :], AX.X, ALU.add))
                    pk.settle(tell=rs_reduced)
                sc.leave(NG)
                pk.leave(NG)

            def dot_pass(q):
                dve.wait_ge(dots_spread, 16 * q)
                dt_ = Steps(dve, piece_scanned[q], carrier["dve"])
                dt_.base = SCAN[q] * SLOTS
                with dve.Fori(0, NG) as g:
                    dt_.enter(g, TPG * NPC)
                    st.enter(g, 1)
                    for c in range(NPC):
                        dve.wait_ge(piece_loaded[c % SLOTS], g * (16 * K4) + 16 * (q * NG * K4 + c // SLOTS + 1))
                        dve.sem_inc(carrier["dve"], 1)
                        for r in range(TPG):
                            if c or r >= 2:
                                dt_.settle(dt_.k - 1)
                            dt_.mark(v.tensor_tensor_reduce(
                                out=junk[r % 2][:, :], in0=pieces[c % SLOTS][:, r, :], in1=D[:, c * PIECE:(c + 1) * PIECE],
                                scale=1.0, scalar=0.0, op0=ALU.mult, op1=ALU.add, accum_out=dp_part[:, r, c:c + 1]))
                    dt_.settle()
                    mark(v.tensor_reduce(tiles_of(DEN[:, :], g), dp_part[:, :, :], AX.X, ALU.add))
                    settle()
                dt_.leave(NG)
                st.leave(NG)
                dve.wait_ge(nat_copied, (q + 1) * NG + 1)

            def general_form():
                STEPS = 3 * ROUNDS + 1
                any_general = dve.value_load(CTL[0:1, 2, 0:1], min_val=0, max_val=1)
                with dve.If(any_general > 0):
                    ge = Steps(dve, general_step, carrier["dve"])
                    with dve.Fori(0, NT) as t:
                        general = dve.value_load(CTL[0:1, 1, bass.ds(t, 1)], min_val=0, max_val=1)
                        dve.wait_ge(row_loaded, t * 16 + 16)
                        dve.sem_inc(carrier["dve"], 1)
                        with dve.If(general > 0):
                            ge.enter(t, STEPS)
                            row = PIECES[:, 0:N]
                            for rd in range(ROUNDS):
                                ge.link(v.max(f8[:, :], row))
                                ge.link(v.max_index(fidx[:, rd * 8:rd * 8 + 8], f8[:, :], row))
                                if rd + 1 < ROUNDS:
                                    ge.link(v.match_replace(row, f8[:, :], row, -3.0e38))
                            ge.mark(v.tensor_copy(IDX[:, bass.ds(t, 1), 1:NGATHER], fidx[:, :].unsqueeze(1)))
                            ge.mark(v.tensor_copy(IDX[:, bass.ds(t, 1), 0], fidx[:, 0:1]))
                            ge.settle(tell=row_used)
                        with dve.Else():
                            dve.sem_inc(general_step, STEPS)
                            dve.sem_inc(row_used, 1)

            def reduce_gathers(par, n, cuts):
                def reduce():
                    v.tensor_reduce(gmax[:, :], ring[par][:, 0:cuts[0], :].rearrange("p k f -> p f k"),
                                    AX.X, ALU.max).then_inc(gather_step, 1)
                if len(cuts) == 1:
                    reduce()
                    return
                with dve.If(n < cuts[0] + 1):
                    reduce()
                with dve.Else():
                    reduce_gathers(par, n, cuts[1:])

            def add_expmap(least):
                squares(2)
                link(v.tensor_scalar(S(2), S(2), least, None, ALU.max))
                ask()
                ask()
                link(v.reciprocal(S(2), S(2)))
                link(v.tensor_tensor(S(3), S(3), S(2), ALU.mult))
                link(v.tensor_tensor(AGG[:, :, :], AGG[:, :, :], by_row(S(3)), ALU.mult))
                link(v.tensor_tensor(X[:, :, :], X[:, :, :], AGG[:, :, :], ALU.add))

            def give_pieces(q):
                dve.sem_inc(piece_scanned[q], SCAN[q] * SLOTS)

            sc = Steps(dve, piece_scanned[0], carrier["dve"])
            pk = Steps(dve, pick_step, carrier["dve"])
            give_pieces(0)
            dve.sem_inc(rs_reduced, 1)
            dve.sem_inc(row_used, 1)
            sc.base = SCAN[0] * SLOTS
            dve.wait_ge(s_load, LOADS)
            dve.wait_ge(ident_ready, 2)
            link(v.tensor_scalar(alph[:, 1:2], alph[:, 0:1], -1.0, 1.0, ALU.mult, ALU.add))
            layernorm()
            project(0, H)
            dve.sem_inc(pass_ready, 1)
            scan_pass()
            dve.sem_inc(flags_ready, 1)
            dve.wait_ge(nat_copied, NG + 1)
            link(v.tensor_scalar(S(2), RS[:, :], alph[:, 0:1], alph[:, 1:2], ALU.mult, ALU.add))
            link(v.tensor_scalar(S(3), S(2), 0.0, None, ALU.is_equal))
            link(v.tensor_tensor(S(2), S(2), S(3), ALU.add))
            link(v.reciprocal(S(2), S(2)))
            link(v.tensor_scalar(S(3), S(3), -1.0, 1.0, ALU.mult, ALU.add))
            link(v.tensor_tensor(S(2), S(2), S(3), ALU.mult))
            ask()
            link(v.scalar_tensor_tensor(AGG[:, :, :], AGG[:, :, :], alph[:, 0:1], H[:, :, :], ALU.mult, ALU.add))
            link(v.tensor_tensor(AGG[:, :, :], AGG[:, :, :], by_row(S(2)), ALU.mult))
            link(v.tensor_tensor(AGG[:, :, :], AGG[:, :, :], by_feature(0), ALU.add))
            link(v.scalar_tensor_tensor(X[:, :, :], AGG[:, :, :], 0.0, X[:, :, :], ALU.max, ALU.add))

            dve.wait_ge(flags_reduced, 1)
            link(v.tensor_scalar(ctlf[:, 1, :], FLAGR[0:1, 1, :], 0.0, None, ALU.is_gt))
            link(v.tensor_scalar(ctlf[:, 0, :], ctlf[:, 1, :], float(NGATHER), None, ALU.mult))
            link(v.scalar_tensor_tensor(ctlf[:, 0, :], FLAGR[0:1, 0, :], 1.0, ctlf[:, 0, :], ALU.add, ALU.max))
            link(v.tensor_scalar(CTL[:, 0, :], ctlf[:, 0, :], float(NGATHER), None, ALU.min))
            link(v.tensor_copy(CTL[:, 1, :], ctlf[:, 1, :]))
            link(v.tensor_reduce(CTL[:, 2, 0:1], ctlf[:, 1, :], AX.X, ALU.max), tell=ctl_ready)
            general_form()
            give_pieces(1)

            layernorm()
            squares(2)
            project(1, H)
            squares(3)
            link(v.tensor_scalar(S(4), S(3), 0.0, None, ALU.add))
            link(v.tensor_scalar(sm[:, 2:4, :], sm[:, 2:4, :], 1e-30, None, ALU.max))
            ask()
            link(v.tensor_scalar(S(5), S(2), 1.0 - 1e-5, None, ALU.min))
            artanh(S(6), S(5))
            link(v.reciprocal(S(7), S(2)))
            link(v.tensor_tensor(S(5), S(3), S(7), ALU.mult))
            link(v.tensor_tensor(S(5), S(5), S(6), ALU.mult))
            ask()
            link(v.reciprocal(S(7), S(3)))
            link(v.tensor_tensor(S(7), S(7), S(5), ALU.mult))
            link(v.tensor_tensor(S(6), S(7), S(7), ALU.mult))
            link(v.tensor_tensor(S(6), S(6), S(4), ALU.mult))
            link(v.tensor_scalar(S(6), S(6), -1.0, 1.0, ALU.mult, ALU.add))
            link(v.tensor_scalar(S(6), S(6), 1e-5, None, ALU.max))
            link(v.reciprocal(S(6), S(6)))
            link(v.tensor_scalar(dots[:, :], S(6), 2.0, -1.0, ALU.mult, ALU.add), tell=dots_small)
            link(v.scalar_tensor_tensor(S(7), S(6), 2.0, S(7), ALU.mult, ALU.mult))
            link(v.tensor_tensor(H[:, :, :], AGG[:, :, :], by_row(S(7)), ALU.mult), tell=pass_ready)
            dot_pass(1)
            link(v.tensor_scalar(S(5), DEN[:, :], 1e-10, None, ALU.max))
            link(v.tensor_scalar(S(6), DEN[:, :], -1e-10, None, ALU.min))
            link(v.tensor_scalar(S(7), DEN[:, :], 0.0, None, ALU.is_ge))
            link(v.tensor_tensor(S(5), S(5), S(6), ALU.subtract))
            link(v.tensor_tensor(S(5), S(5), S(7), ALU.mult))
            link(v.tensor_tensor(S(5), S(5), S(6), ALU.add))
            link(v.reciprocal(S(8), S(5)))
            squares(2)
            link(v.tensor_tensor(S(2), S(2), S(8), ALU.mult))
            link(v.tensor_tensor(S(2), S(2), S(8), ALU.mult))
            link(v.tensor_scalar(S(2), S(2), 1e-30, None, ALU.max))
            ask()
            link(v.tensor_scalar(S(3), S(2), 1.0 - 1e-5, None, ALU.min))
            artanh(S(4), S(3))
            ask()
            link(v.reciprocal(S(2), S(2)))
            link(v.tensor_tensor(S(8), S(8), S(2), ALU.mult))
            link(v.tensor_scalar(S(5), S(4), 1e-15, None, ALU.max))
            link(v.reciprocal(S(7), S(5)))
            link(v.tensor_tensor(S(4), S(4), S(7), ALU.mult))
            link(v.tensor_scalar(S(3), S(5), 1.0 - 1e-5, None, ALU.min))
            artanh(S(6), S(3))
            link(v.tensor_tensor(S(6), S(6), RS[:, :], ALU.mult))
            ask()
            link(v.tensor_tensor(S(6), S(6), S(4), ALU.mult))
            link(v.tensor_tensor(S(8), S(8), S(6), ALU.mult))
            link(v.tensor_scalar(S(5), S(6), -1.0, None, ALU.mult))
            link(v.tensor_tensor(S(5), S(5), S(6), ALU.max))
            link(v.tensor_scalar(S(5), S(5), 1e-15, None, ALU.max))
            link(v.tensor_scalar(S(3), S(5), 1.0 - 1e-5, None, ALU.min))
            artanh(S(4), S(3))
            link(v.reciprocal(S(5), S(5)))
            link(v.tensor_tensor(S(8), S(8), S(4), ALU.mult))
            link(v.tensor_tensor(S(8), S(8), S(5), ALU.mult))
            link(v.tensor_tensor(AGG[:, :, :], AGG[:, :, :], by_row(S(8)), ALU.mult))
            link(v.tensor_scalar(AGG[:, :, :], AGG[:, :, :], 0.0, None, ALU.max))
            add_expmap(1e-30)

            layernorm()
            project(2, H)
            link(v.tensor_tensor(AGG[:, :, :], AGG[:, :, :], by_feature(1), ALU.add), tell=h_ready)
            dve.wait_ge(prefix_copied, 1)
            link(v.tensor_tensor_scan(pfx[:, 1, :], pfx[:, 0, :], pfx[:, 0, :], -3.0e38, ALU.max, ALU.max),
                 tell=prefix_scanned)
            gr = Steps(dve, gather_step, carrier["dve"])
            for par in range(2):
                gr.link(v.tensor_copy(idx_now[par][:, :], IDX[:, par, :]), tell=idx_staged)
            with dve.Fori(0, NT // 2) as i:
                gr.enter(i, 6)
                for par in range(2):
                    n = dve.value_load(CTL[0:1, 0, bass.ds(i * 2 + par, 1)], min_val=1, max_val=NGATHER)
                    dve.wait_ge(gathered[par], i * FULL + FULL)
                    dve.sem_inc(carrier["dve"], 1)
                    reduce_gathers(par, n, CUTS)
                    gr.k += 1
                    gr.settle()
                    t = i * 2 + par
                    gr.mark(v.tensor_tensor(X[:, bass.ds(t, 1), :], X[:, bass.ds(t, 1), :],
                                            gmax[:, :].unsqueeze(1), ALU.add))
                    gr.mark(v.tensor_copy(idx_now[par][:, :], IDX[:, bass.ds(t + 2, 1), :]))
                    gr.settle(tell=idx_staged)
            gr.leave(NT // 2)
            give_pieces(2)

            layernorm()
            squares(2)
            link(v.tensor_scalar(S(2), S(2), -1.0, 1.0, ALU.mult, ALU.add))
            link(v.reciprocal(S(2), S(2)))
            link(v.tensor_scalar(S(7), S(2), 2.0, 1e7, ALU.mult, ALU.min))
            link(v.tensor_scalar(S(3), RS[:, :], 1.0, None, ALU.add))
            ask()
            link(v.reciprocal(dots[:, :], S(3)), tell=dots_small)
            link(v.tensor_tensor(H[:, :, :], H[:, :, :], by_row(dots[:, :]), ALU.mult), tell=pass_ready)
            dot_pass(2)
            link(v.tensor_tensor(S(5), DEN[:, :], dots[:, :], ALU.add))
            link(v.scalar_tensor_tensor(S(5), S(7), -1.0, S(5), ALU.add, ALU.mult))
            link(v.reciprocal(S(5), S(5)))
            link(v.tensor_tensor(S(5), S(5), S(7), ALU.mult))
            link(v.tensor_tensor(AGG[:, :, :], AGG[:, :, :], H[:, :, :], ALU.add))
            link(v.tensor_tensor(AGG[:, :, :], AGG[:, :, :], by_row(S(5)), ALU.mult))
            squares(2)
            link(v.tensor_scalar(S(2), S(2), 1e-30, None, ALU.max))
            ask()
            link(v.tensor_scalar(S(3), S(2), 1e-7, 1.0 - 1e-7, ALU.max, ALU.min))
            artanh(S(4), S(3))
            ask()
            link(v.reciprocal(S(5), S(3)))
            link(v.tensor_tensor(S(8), S(4), S(5), ALU.mult))
            link(v.tensor_tensor(S(3), S(2), S(8), ALU.mult))
            link(v.tensor_scalar(S(3), S(3), 1e-7, 1.0 - 1e-7, ALU.max, ALU.min))
            artanh(S(4), S(3))
            link(v.reciprocal(S(3), S(3)))
            link(v.tensor_tensor(S(8), S(8), S(4), ALU.mult))
            link(v.tensor_tensor(S(8), S(8), S(3), ALU.mult))
            link(v.tensor_tensor(H[:, :, :], AGG[:, :, :], by_row(S(8)), ALU.mult))
            project(3, H)
            link(v.tensor_tensor(AGG[:, :, :], AGG[:, :, :], by_feature(2), ALU.add))
            link(v.tensor_scalar(AGG[:, :, :], AGG[:, :, :], 0.0, None, ALU.max))
            add_expmap(1e-14)
            dve.sem_inc(x_done, 1)


_INS = ["x", "adj", "L0_gnn_alpha", "L0_gnn_W", "L0_gnn_b", "L1_gnn_W", "L2_gnn_W", "L2_gnn_b", "L3_gnn_W",
        "L3_gnn_b"]


def kernel(**inputs):
    import numpy as np
    import concourse.bacc as bacc
    from concourse.bass_utils import run_bass_kernel_spmd

    nc = bacc.Bacc("TRN2", target_bir_lowering=False, num_devices=1)
    arrays, args = {}, []
    for name in _INS:
        a = np.ascontiguousarray(inputs[name])
        arrays[f"in_{name}"] = a
        args.append(nc.dram_tensor(f"in_{name}", a.shape, mybir.dt.from_np(a.dtype), kind="ExternalInput").ap())
    out = nc.dram_tensor("out_x", inputs["x"].shape, mybir.dt.float32, kind="ExternalOutput").ap()
    build(nc, *args, out)
    r = run_bass_kernel_spmd(nc, [arrays], core_ids=[0])
    return r.results[0]["out_x"]
```

```python
import concourse.bass as bass
from concourse import mybir
from contextlib import ExitStack

P = 128
TPG = 4
GROUP = TPG * P
PIECE = 512
SLOTS = 4
TOPK = 32
PREFIX = 64
NGATHER = TOPK
COMMON = 14
CUTS = [16, 17, 18, 19, 20, 21, 23, 26, NGATHER]
ROUNDS = TOPK // 8
NAT = 4
LN_EPS = 1e-5

fp32 = mybir.dt.float32
u32 = mybir.dt.uint32
i32 = mybir.dt.int32
ALU = mybir.AluOpType
ACT = mybir.ActivationFunctionType
AX = mybir.AxisListType
RMAX = bass.bass_isa.ReduceOp.max


class Steps:

    def __init__(self, engine, semaphore, carrier):
        self.engine, self.semaphore, self.carrier = engine, semaphore, carrier
        self.base, self.turn, self.per, self.k = 0, None, 0, 0

    def value(self, k):
        return self.base + k if self.turn is None else self.turn * self.per + (self.base + k)

    def mark(self, instruction):
        instruction.then_inc(self.semaphore, 1)
        self.k += 1
        return self.k

    def settle(self, k=None, tell=None):
        self.engine.wait_ge(self.semaphore, self.value(self.k if k is None else k))
        if tell is not None:
            self.engine.sem_inc(tell, 1)
        elif self.turn is not None:
            self.engine.sem_inc(self.carrier, 1)

    def link(self, instruction, tell=None):
        self.mark(instruction)
        self.settle(tell=tell)

    def enter(self, turn, per):
        self.base, self.turn, self.per, self.k = self.base + self.k, turn, per, 0

    def leave(self, turns):
        assert self.k == self.per, (self.k, self.per)
        self.base, self.turn, self.k = self.base + turns * self.per, None, 0


def build(nc, x, adj, alpha, w0, b0, w1, w2, b2, w3, b3, out):
    N = x.shape[0]
    NT = N // P
    NG = NT // TPG
    NPC = N // PIECE
    BPP = PIECE // P
    NP = NT // 2
    K4 = NPC // SLOTS
    assert NG % 2 == 0 and NPC % SLOTS == 0

    x_v = x.rearrange("(t p) f -> p t f", p=P)
    out_v = out.rearrange("(t p) f -> p t f", p=P)
    adj_v = adj.rearrange("(g r p) (c x) -> g c p r x", p=P, r=TPG, x=PIECE)
    adj_rows = adj.rearrange("(t p) n -> t p n", p=P)
    table = nc.dram_tensor("h_table", (N + PREFIX, P), fp32).ap()
    turned = nc.dram_tensor("adj_turned", (NG, NP, P, 2 * GROUP), fp32).ap()
    turned_v = turned.rearrange("g (c k) p x -> g c p k x", k=2)

    ctx = ExitStack()
    with ctx:
        def sb(name, shape, dt=fp32):
            return ctx.enter_context(nc.sbuf_tensor(name, shape, dt))

        def pb(name, shape):
            return ctx.enter_context(nc.psum_tensor(name, shape, fp32))

        def sem(name):
            return ctx.enter_context(nc.semaphore(name))

        X = sb("X", [P, NT, P])
        H = sb("H", [P, NT, P])
        AGG = sb("AGG", [P, NT, P])
        D = sb("D", [P, max(N, 2 * NGATHER * P)])
        PIECES = sb("PIECES", [P, max(SLOTS * TPG * PIECE, N)])
        ATS = sb("ATS", [P, NAT, 2 * GROUP])
        AT = [ATS[:, i, :] for i in range(NAT)]
        aggT = sb("aggT", [P, GROUP])
        gmax = sb("gmax", [P, P])
        ident = sb("ident", [P, P])
        wnat = sb("wnat", [P, 2, P])
        W = [sb(f"W{i}", [P, P]) for i in range(4)]
        bias = sb("bias", [P, 3, P])
        alph = sb("alph", [P, 2])
        IDX = sb("IDX", [P, NT + 2, NGATHER], mybir.dt.uint16)
        idx_now = [sb(f"idx_now{i}", [P, NGATHER], u32) for i in range(2)]
        rs_part = sb("rs_part", [P, TPG, NPC])
        RS = sb("RS", [P, NT])
        DEN = sb("DEN", [P, NT])
        FLAGS = sb("FLAGS", [P, 2, NT])
        FLAGR = sb("FLAGR", [P, 2, NT])
        CTL = sb("CTL", [1, 3, NT], i32)
        ctlf = sb("ctlf", [1, 2, NT])
        sm = sb("sm", [P, 14, NT])
        dots = sb("dots", [P, NT])
        ones_col = sb("ones_col", [P, 1])
        s4 = sb("s4", [P, 10, TPG])
        f8 = sb("f8", [P, 8])
        fidx = sb("fidx", [P, TOPK], u32)
        pfx = sb("pfx", [P, 2, PREFIX])
        pfxn = sb("pfxn", [PREFIX, P])

        pieces = [PIECES[:, i * TPG * PIECE:(i + 1) * TPG * PIECE].rearrange("p (r x) -> p r x", r=TPG)
                  for i in range(SLOTS)]
        SQ = D[:, 0:N].rearrange("p (t f) -> p t f", f=P)
        pieces_t = [PIECES[:, i * TPG * PIECE:(i + 1) * TPG * PIECE].rearrange("p (b x) -> p b x", b=BPP)
                    for i in range(SLOTS)]
        ring = [D[:, i * NGATHER * P:(i + 1) * NGATHER * P].rearrange("p (k f) -> p k f", f=P) for i in range(2)]
        dacc = ATS[:, 0:2, :].rearrange("p k (b x) -> p (k b) x", b=2)
        CW = NPC * 8
        at = [0]

        def part(n):
            at[0] += n
            assert at[0] <= D.shape[1]
            return D[:, at[0] - n:at[0]]

        cand = part(TPG * CW).rearrange("p (r c e) -> p r c e", r=TPG, e=8)
        cidx = part(TPG * CW).bitcast(u32).rearrange("p (r c e) -> p r c e", r=TPG, e=8)
        cbase = part(TPG * CW).rearrange("p (r c e) -> p r c e", r=TPG, e=8)
        pos = part(TPG * CW).rearrange("p (r c e) -> p r c e", r=TPG, e=8)
        keys = part(TPG * CW).rearrange("p (r k) -> p r k", r=TPG)
        zero = part(TPG * PREFIX).rearrange("p (r k) -> p r k", r=TPG)
        zcum = part(TPG * PREFIX).rearrange("p (r k) -> p r k", r=TPG)
        ones = part(PREFIX)
        top = part(TPG * TOPK).rearrange("p (r k) -> p r k", r=TPG)
        topm = part(TPG * TOPK).rearrange("p (r k) -> p r k", r=TPG)
        topd = part(TPG * TOPK).rearrange("p (r k) -> p r k", r=TPG)

        psT = [pb(f"psT{i}", [P, 2 * GROUP]) for i in range(2)]
        psA = pb("psA", [P, GROUP])
        psN = pb("psN", [P, GROUP])
        psX = pb("psX", [P, GROUP])
        psY = pb("psY", [P, GROUP])
        junk = [psX, psY]

        s_load = sem("s_load")
        s_ident = sem("s_ident")
        ident_ready = sem("ident_ready")
        pick_constants = sem("pick_constants")
        prefix_copied = sem("prefix_copied")
        weights_transposed = sem("weights_transposed")
        carrier = {e: sem(f"carrier_{e}") for e in ("dve", "act", "pe", "sp", "pool")}
        dve_step = sem("dve_step")
        pick_step = sem("pick_step")
        act_step = sem("act_step")
        piece_loaded = [sem(f"piece_loaded{i}") for i in range(SLOTS)]
        pass_ready = sem("pass_ready")
        pair_transposed = [sem("pair_transposed")]
        piece_scanned = [sem(f"piece_scanned{q}") for q in range(3)]
        piece_summed = sem("piece_summed")
        pair_copied = sem("pair_copied")
        pair_used = sem("pair_used")
        acc_copied = sem("acc_copied")
        nat_ready = sem("nat_ready")
        nat_copied = sem("nat_copied")
        rs_reduced = sem("rs_reduced")
        flags_ready = sem("flags_ready")
        flags_reduced = sem("flags_reduced")
        ctl_ready = sem("ctl_ready")
        row_loaded = sem("row_loaded")
        row_used = sem("row_used")
        general_step = sem("general_step")
        for_act = sem("for_act")
        from_act = sem("from_act")
        proj_start = sem("proj_start")
        staged = sem("staged")
        stage_read = sem("stage_read")
        hT_copied = sem("hT_copied")
        projected = sem("projected")
        proj_out = sem("proj_out")
        pair_stored = [sem(f"pair_stored{i}") for i in range(NAT)]
        pair_free = sem("pair_free")
        turned_stored = sem("turned_stored")
        piece_multiplied = [sem(f"piece_multiplied{q}") for q in (1, 2)]
        dots_summed = sem("dots_summed")
        den_ready = sem("den_ready")
        den_step = sem("den_step")
        h_ready = sem("h_ready")
        prefix_t = sem("prefix_t")
        prefix_scanned = sem("prefix_scanned")
        prefix_n = sem("prefix_n")
        prefix_ready = sem("prefix_ready")
        table_stored = sem("table_stored")
        idx_staged = sem("idx_staged")
        gathered = [sem(f"gathered{i}") for i in range(2)]
        reduced = sem("reduced")
        gather_step = sem("gather_step")
        x_done = sem("x_done")
        s_out = sem("s_out")

        block = ctx.enter_context(nc.Block())
        LOADS = 9 * 16
        PICK = 22 + 2 * ROUNDS * TPG
        SCAN = [2 * TPG, TPG, TPG]
        FULL = 16 * NGATHER

        def tiles_of(A, g):
            return A[:, bass.ds(g * TPG, TPG)]

        @block.sync
        def _(sp):
            sp.dma_start(X[:, :, :], x_v).then_inc(s_load, 16)
            sp.dma_start(wnat[:, 0, :], w0).then_inc(s_load, 16)
            sp.dma_start(wnat[:, 1, :], w2).then_inc(s_load, 16)
            sp.dma_start(W[1][:, :], w1).then_inc(s_load, 16)
            sp.dma_start(W[3][:, :], w3).then_inc(s_load, 16)
            for n, b in enumerate((b0, b2, b3)):
                sp.dma_start(bias[:, n, :], b.partition_broadcast(P)).then_inc(s_load, 16)
            sp.dma_start(alph[:, 0:1], alpha.partition_broadcast(P)).then_inc(s_load, 16)

            def load_pieces(q):
                with sp.Fori(0, NG) as g:
                    for c in range(NPC):
                        sp.wait_ge(pair_transposed[q], g * (2 * NPC) + 2 * (c + 1))
                        sp.sem_inc(carrier["sp"], 1)
                        sp.wait_ge(piece_scanned[q], g * (NPC * SCAN[q]) + SCAN[q] * (c + 1))
                        if q == 0:
                            sp.sem_inc(carrier["sp"], 1)
                            sp.wait_ge(piece_summed, g * NPC + (c + 1))
                        sp.sem_inc(carrier["sp"], 1)
                        sp.dma_start(pieces[c % SLOTS], adj_v[bass.ds(g, 1), c, :, :, :])\
                          .then_inc(piece_loaded[c % SLOTS], 16)

            def load_turned(q):
                with sp.Fori(0, NG) as g:
                    for c in range(NPC):
                        sp.wait_ge(piece_multiplied[q - 1], g * NPC + (c + 1))
                        sp.sem_inc(carrier["sp"], 1)
                        sp.wait_ge(piece_scanned[q], g * (NPC * SCAN[q]) + SCAN[q] * (c + 1))
                        sp.sem_inc(carrier["sp"], 1)
                        sp.dma_start(PIECES[:, (c % SLOTS) * TPG * PIECE:(c % SLOTS + 1) * TPG * PIECE]
                                     .rearrange("p (k x) -> p k x", k=2), turned_v[bass.ds(g, 1), c, :, :, :])\
                          .then_inc(piece_loaded[c % SLOTS], 16)

            load_pieces(0)

            sp.wait_ge(ctl_ready, 1)
            any_general = sp.value_load(CTL[0:1, 2, 0:1], min_val=0, max_val=1)
            with sp.If(any_general > 0):
                with sp.Fori(0, NT) as t:
                    general = sp.value_load(CTL[0:1, 1, bass.ds(t, 1)], min_val=0, max_val=1)
                    sp.wait_ge(row_used, t + 1)
                    sp.sem_inc(carrier["sp"], 1)
                    with sp.If(general > 0):
                        sp.dma_start(PIECES[:, 0:N], adj_rows[bass.ds(t, 1), :, :]).then_inc(row_loaded, 16)
                    with sp.Else():
                        sp.dma_start(PIECES[0:16, 0:8], adj_rows[0, 0:16, 0:8]).then_inc(row_loaded, 16)

            sp.wait_ge(turned_stored, 1)
            load_turned(1)

            sp.wait_ge(h_ready, 1)
            sp.dma_start(table[0:N, :].rearrange("(t p) f -> p t f", p=P), AGG[:, :, :]).then_inc(table_stored, 16)
            sp.wait_ge(prefix_ready, 1)
            sp.dma_start(table[N:N + PREFIX, :], pfxn[:, :]).then_inc(table_stored, 16)

            load_turned(2)

            sp.wait_ge(x_done, 1)
            sp.dma_start(out_v, X[:, :, :]).then_inc(s_out, 16)
            sp.wait_ge(s_out, 16)
            sp.wait_ge(table_stored, 32)

        @block.gpsimd
        def _(pool):
            pool.memset(ident[:, :], 0.0).then_inc(s_ident, 1)
            pool.wait_ge(s_ident, 1)
            pool.affine_select(out=ident[:, :], in_=ident[:, :], compare_op=ALU.not_equal, fill=1.0,
                               base=0, pattern=[[-1, P]], channel_multiplier=1).then_inc(ident_ready, 1)
            pool.memset(IDX[:, NT:NT + 2, :], 0).then_inc(ident_ready, 1)
            pool.wait_ge(pass_ready, 1)
            pool.memset(ones, 1.0).then_inc(pick_constants, 1)
            pool.iota(cbase, [[0, TPG], [PIECE, NPC], [0, 8]], base=1, channel_multiplier=0,
                      allow_small_or_imprecise_dtypes=True).then_inc(pick_constants, 1)

            pool.sem_inc(pair_free, NAT)
            with pool.Fori(0, NG) as g:
                def landed(k):
                    pool.wait_ge(pair_stored[k % NAT], g * (16 * (NP // NAT)) + 16 * (k // NAT + 1))
                    pool.sem_inc(pair_free, 1)

                for k in range(NP):
                    pool.wait_ge(pair_copied, g * NP + (k + 1 + 2))
                    pool.sem_inc(carrier["pool"], 1)
                    pool.dma_start(turned[bass.ds(g, 1), k, :, :], AT[k % NAT]).then_inc(pair_stored[k % NAT], 16)
                    if k >= 2:
                        landed(k - 2)
                landed(NP - 2)
                landed(NP - 1)
            pool.sem_inc(turned_stored, 1)

            pool.wait_ge(flags_ready, 1)
            pool.partition_all_reduce(FLAGR[:, :, :].rearrange("p a t -> p (a t)"),
                                      FLAGS[:, :, :].rearrange("p a t -> p (a t)"), P, RMAX)\
                .then_inc(flags_reduced, 1)

            def gather(par, k, inc):
                pool.indirect_dma_start(ring[par][:, k, :], None, table,
                                        bass.IndirectOffsetOnAxis(ap=idx_now[par][:, k:k + 1], axis=0))\
                    .then_inc(gathered[par], inc)

            def gathers(par, n, cuts):
                def leaf(count):
                    for k in range(COMMON, count):
                        share = (NGATHER - COMMON) * (k + 1 - COMMON) // (count - COMMON) - \
                            (NGATHER - COMMON) * (k - COMMON) // (count - COMMON)
                        gather(par, k, 16 * share)
                if len(cuts) == 1:
                    leaf(cuts[0])
                    return
                with pool.If(n < cuts[0] + 1):
                    leaf(cuts[0])
                with pool.Else():
                    gathers(par, n, cuts[1:])

            pool.wait_ge(ctl_ready, 1)
            pool.wait_ge(table_stored, 32)
            with pool.Fori(0, NT // 2) as i:
                for par in range(2):
                    n = pool.value_load(CTL[0:1, 0, bass.ds(i * 2 + par, 1)], min_val=1, max_val=NGATHER)
                    pool.wait_ge(idx_staged, i * 2 + (par + 1))
                    pool.sem_inc(carrier["pool"], 1)
                    for k in range(COMMON):
                        gather(par, k, 16)
                    gathers(par, n, CUTS)

        @block.tensor
        def _(pe):
            pe.wait_ge(s_load, LOADS)
            pe.wait_ge(ident_ready, 2)
            nc.tensor.transpose(psX[:, 0:P], wnat[:, 0, :], ident[:, :])
            nc.tensor.transpose(psX[:, P:2 * P], wnat[:, 1, :], ident[:, :]).then_inc(weights_transposed, 1)

            def project(n, w):
                with pe.Fori(0, NG // 2) as i:
                    for h in range(2):
                        pe.wait_ge(staged, i * 2 + (n * NG + h + 1))
                        for r in range(TPG):
                            last = nc.tensor.transpose(psT[h][:, r * P:(r + 1) * P],
                                                       AT[h][:, r * P:(r + 1) * P], ident[:, :])
                        last.then_inc(stage_read, 1)
                    for h, ps in enumerate((psX, psY)):
                        pe.wait_ge(hT_copied, i * 2 + (n * NG + h + 1))
                        pe.wait_ge(proj_out, i * 2 + (n * NG + h + 1))
                        for r in range(TPG):
                            last = nc.tensor.matmul(ps[:, r * P:(r + 1) * P],
                                                    AT[h][:, GROUP + r * P:GROUP + (r + 1) * P], W[w][:, :],
                                                    start=True, stop=True)
                        last.then_inc(projected, 1)

            def turn_back(g, q):
                pe.wait_ge(acc_copied, g + (q * NG + 2))
                pe.wait_ge(nat_copied, g + (q * NG + 1))
                for r in range(TPG):
                    last = nc.tensor.transpose(psN[:, r * P:(r + 1) * P], aggT[:, r * P:(r + 1) * P], ident[:, :])
                last.then_inc(nat_ready, 1)

            def turned_pass(q):
                pe.wait_ge(pass_ready, q + 1)
                with pe.Fori(0, NG) as g:
                    for c in range(NPC):
                        pe.wait_ge(piece_loaded[c % SLOTS], g * (16 * K4) + 16 * (q * NG * K4 + c // SLOTS + 1))
                        if c == 0:
                            pe.wait_ge(acc_copied, g + (q * NG + 1))
                        for b in range(BPP):
                            j = BPP * c + b
                            last = nc.tensor.matmul(psA[:, :], H[:, j, :], pieces_t[c % SLOTS][:, b, :],
                                                    start=(j == 0), stop=(j == NT - 1))
                        last.then_inc(piece_multiplied[q - 1], 1)
                    turn_back(g, q)
                    pe.wait_ge(dots_summed, g + ((q - 1) * NG + 1))
                    pe.wait_ge(den_step, g + ((q - 1) * NG + 1))
                    for r in range(TPG):
                        last = nc.tensor.matmul(psX[:, r:r + 1], dacc[:, 0, r * P:(r + 1) * P], ones_col[:, :],
                                                start=True, stop=True)
                    last.then_inc(den_ready, 1)

            def adjacency_pass(q):
                pe.wait_ge(pass_ready, q + 1)
                with pe.Fori(0, NG) as g:
                    def turn_pair(k):
                        if k % 2 == 0:
                            c = k // 2
                            pe.wait_ge(piece_loaded[c % SLOTS], g * (16 * K4) + 16 * (q * NG * K4 + c // SLOTS + 1))
                        pe.wait_ge(pair_copied, g * NP + (q * NG * NP + k + 1))
                        for b in range(2):
                            x0 = (k % 2) * 2 * P + b * P
                            for r in range(TPG):
                                last = nc.tensor.transpose(psT[k % 2][:, b * GROUP + r * P:b * GROUP + (r + 1) * P],
                                                           pieces[(k // 2) % SLOTS][:, r, x0:x0 + P], ident[:, :])
                        last.then_inc(pair_transposed[q], 1)

                    turn_pair(0)
                    for k in range(NP):
                        if k + 1 < NP:
                            turn_pair(k + 1)
                        pe.wait_ge(pair_copied, g * NP + (q * NG * NP + k + 1 + 2))
                        if k == 0:
                            pe.wait_ge(acc_copied, g + (q * NG + 1))
                        for b in range(2):
                            j = 2 * k + b
                            last = nc.tensor.matmul(psA[:, :], H[:, j, :], AT[k % NAT][:, b * GROUP:(b + 1) * GROUP],
                                                    start=(j == 0), stop=(j == NT - 1))
                        last.then_inc(pair_used, 1)
                    turn_back(g, q)

            pe.sem_inc(pair_transposed[0], 2 * SLOTS)
            pe.sem_inc(pair_used, NAT)
            pe.sem_inc(piece_multiplied[0], SLOTS)
            pe.sem_inc(stage_read, 2)
            pe.sem_inc(nat_ready, 1)
            pe.sem_inc(projected, 2)
            project(0, 0)
            adjacency_pass(0)
            project(1, 1)
            turned_pass(1)
            pe.sem_inc(piece_multiplied[1], SLOTS)
            project(2, 2)
            pe.wait_ge(h_ready, 1)
            nc.tensor.transpose(psX[:, 0:PREFIX], AGG[0:PREFIX, 0, :], ident[0:PREFIX, 0:PREFIX]).then_inc(prefix_t, 1)
            pe.wait_ge(prefix_scanned, 1)
            nc.tensor.transpose(psY[0:PREFIX, 0:P], pfx[:, 1, :], ident[:, :]).then_inc(prefix_n, 1)
            turned_pass(2)
            project(3, 3)

        @block.scalar
        def _(act):
            st = Steps(act, act_step, carrier["act"])
            asked = [0]

            def job(out, in_, func, **kw):
                asked[0] += 1
                act.wait_ge(for_act, asked[0])
                nc.scalar.activation(out, in_, func, **kw).then_inc(from_act, 1)

            def project(n, dest):
                with act.Fori(0, NG // 2) as i:
                    for h in range(2):
                        act.wait_ge(stage_read, i * 2 + (n * NG + h + 1 + 2))
                        act.wait_ge(projected, i * 2 + (n * NG + h + 1))
                        act.sem_inc(carrier["act"], 1)
                        nc.scalar.activation(AT[h][:, GROUP:2 * GROUP], psT[h][:, 0:GROUP], ACT.Copy)\
                            .then_inc(hT_copied, 1)
                    for h, ps in enumerate((psX, psY)):
                        act.wait_ge(projected, i * 2 + (n * NG + h + 1 + 2))
                        act.sem_inc(carrier["act"], 1)
                        nc.scalar.activation(tiles_of(dest, i * 2 + h), ps[:, :], ACT.Copy).then_inc(proj_out, 1)

            def adjacency_pass(q):
                with act.Fori(0, NG) as g:
                    if q == 0:
                        st.enter(g, TPG * NPC)
                    for k in range(NP):
                        act.wait_ge(pair_transposed[q], g * NP + (k + 1 + 2 * SLOTS))
                        act.wait_ge(pair_used, g * NP + (k + 1))
                        act.wait_ge(pair_free, g * NP + (k + 1))
                        nc.scalar.activation(AT[k % NAT], psT[k % 2][:, :], ACT.Copy).then_inc(pair_copied, 1)
                        if q == 0 and k % 2 == 1:
                            c = k // 2
                            if c == 0:
                                act.wait_ge(rs_reduced, g + 1)
                                act.sem_inc(carrier["act"], 1)
                            act.wait_ge(piece_loaded[c % SLOTS], g * (16 * K4) + 16 * (c // SLOTS + 1))
                            act.sem_inc(carrier["act"], 1)
                            for r in range(TPG):
                                if r >= 2:
                                    st.settle(st.k - 1)
                                st.mark(nc.scalar.activation(junk[r % 2][:, :], pieces[c % SLOTS][:, r, :], ACT.Copy,
                                                             accum_out=rs_part[:, r, c:c + 1]))
                            st.settle(tell=piece_summed)
                    act.wait_ge(pair_used, g * NP + (NP + NAT))
                    act.sem_inc(carrier["act"], 1)
                    copy_sums(g, q)
                st.leave(NG)

            def copy_sums(g, q):
                act.wait_ge(nat_ready, g + (q * NG + 1))
                act.sem_inc(carrier["act"], 1)
                nc.scalar.activation(aggT[:, :], psA[:, :], ACT.Copy).then_inc(acc_copied, 1)
                act.wait_ge(nat_ready, g + (q * NG + 2))
                act.sem_inc(carrier["act"], 1)
                nc.scalar.activation(tiles_of(AGG, g), psN[:, :], ACT.Copy).then_inc(nat_copied, 1)

            def turned_pass(q):
                with act.Fori(0, NG) as g:
                    act.wait_ge(piece_multiplied[q - 1], g * NPC + (NPC + SLOTS))
                    act.sem_inc(carrier["act"], 1)
                    copy_sums(g, q)

            def artanh():
                job(sm[:, 13, :], sm[:, 12, :], ACT.Ln)

            def layernorm():
                job(SQ, H[:, :, :], ACT.Square)
                job(sm[:, 1, :], sm[:, 0, :], ACT.Sqrt)

            act.sem_inc(piece_summed, SLOTS)
            act.sem_inc(pair_copied, 2)
            act.sem_inc(acc_copied, 1)
            act.sem_inc(nat_copied, 1)
            act.sem_inc(proj_out, 2)
            act.wait_ge(weights_transposed, 1)
            st.mark(nc.scalar.activation(W[0][:, :], psX[:, 0:P], ACT.Copy))
            st.mark(nc.scalar.activation(W[2][:, :], psX[:, P:2 * P], ACT.Copy))
            st.settle()
            layernorm()
            project(0, H)
            adjacency_pass(0)
            job(H[:, :, :], H[:, :, :], ACT.Copy, scale=alph[:, 1:2])
            layernorm()
            job(SQ, H[:, :, :], ACT.Square)
            project(1, AGG)
            job(SQ, AGG[:, :, :], ACT.Square)
            job(sm[:, 2:4, :], sm[:, 2:4, :], ACT.Sqrt)
            artanh()
            job(sm[:, 5, :], sm[:, 5, :], ACT.Tanh)
            turned_pass(1)
            job(SQ, AGG[:, :, :], ACT.Square)
            job(sm[:, 2, :], sm[:, 2, :], ACT.Sqrt)
            artanh()
            job(sm[:, 4, :], sm[:, 4, :], ACT.Tanh, scale=0.5)
            artanh()
            job(sm[:, 6, :], sm[:, 6, :], ACT.Tanh)
            artanh()
            job(SQ, AGG[:, :, :], ACT.Square)
            job(sm[:, 2, :], sm[:, 2, :], ACT.Sqrt)
            job(sm[:, 3, :], sm[:, 2, :], ACT.Tanh)
            layernorm()
            project(2, AGG)
            act.wait_ge(prefix_t, 1)
            nc.scalar.activation(pfx[:, 0, :], psX[:, 0:PREFIX], ACT.Copy).then_inc(prefix_copied, 1)
            act.wait_ge(prefix_n, 1)
            nc.scalar.activation(pfxn[:, :], psY[0:PREFIX, 0:P], ACT.Copy).then_inc(prefix_ready, 1)
            layernorm()
            job(SQ, H[:, :, :], ACT.Square)
            job(sm[:, 3, :], sm[:, 3, :], ACT.Sqrt)
            turned_pass(2)
            job(SQ, AGG[:, :, :], ACT.Square)
            job(sm[:, 2, :], sm[:, 2, :], ACT.Sqrt)
            artanh()
            job(sm[:, 4, :], sm[:, 4, :], ACT.Tanh, scale=0.5)
            artanh()
            project(3, AGG)
            job(SQ, AGG[:, :, :], ACT.Square)
            job(sm[:, 2, :], sm[:, 2, :], ACT.Sqrt)
            job(sm[:, 3, :], sm[:, 2, :], ACT.Tanh)

        @block.vector
        def _(dve):
            v = nc.vector
            st = Steps(dve, dve_step, carrier["dve"])
            link, mark, settle = st.link, st.mark, st.settle
            asked = [0]

            def S(k):
                return sm[:, k, :]

            def ask():
                asked[0] += 1
                dve.sem_inc(for_act, 1)
                dve.wait_ge(from_act, asked[0])

            def by_row(a):
                return a.unsqueeze(2).to_broadcast([P, NT, P])

            def by_feature(n):
                return bias[:, n, :].unsqueeze(1).to_broadcast([P, NT, P])

            def layernorm():
                link(v.tensor_reduce(S(0), X[:, :, :], AX.X, ALU.add))
                link(v.tensor_scalar(S(0), S(0), -1.0 / P, None, ALU.mult))
                link(v.tensor_tensor(H[:, :, :], X[:, :, :], by_row(S(0)), ALU.add))
                ask()
                link(v.tensor_reduce(S(0), SQ, AX.X, ALU.add))
                link(v.tensor_scalar(S(0), S(0), 1.0 / P, LN_EPS, ALU.mult, ALU.add))
                ask()
                link(v.reciprocal(S(1), S(1)))
                link(v.scalar_tensor_tensor(H[:, :, :], H[:, :, :], 0.0, by_row(S(1)), ALU.max, ALU.mult))

            def squares(k):
                ask()
                link(v.tensor_reduce(S(k), SQ, AX.X, ALU.add))

            def artanh(out, y):
                a, q, y2, m = S(12), S(11), S(10), S(9)
                link(v.tensor_scalar(q, y, -1.0, 1.0, ALU.mult, ALU.add))
                link(v.reciprocal(q, q))
                link(v.scalar_tensor_tensor(a, y, 1.0, q, ALU.add, ALU.mult))
                ask()
                link(v.tensor_tensor(y2, y, y, ALU.mult))
                link(v.tensor_scalar(q, y2, 1.0 / 13, None, ALU.mult))
                for k in (11, 9, 7, 5, 3):
                    link(v.scalar_tensor_tensor(q, q, 1.0 / k, y2, ALU.add, ALU.mult))
                link(v.scalar_tensor_tensor(q, q, 1.0, y, ALU.add, ALU.mult))
                link(v.tensor_scalar(m, y, 0.25, None, ALU.is_lt))
                link(v.scalar_tensor_tensor(q, S(13), -0.5, q, ALU.mult, ALU.add))
                link(v.tensor_tensor(q, q, m, ALU.mult))
                link(v.scalar_tensor_tensor(out, S(13), 0.5, q, ALU.mult, ALU.add))

            def project(n, src):
                with dve.Fori(0, NG // 2) as i:
                    for h in range(2):
                        dve.wait_ge(stage_read, i * 2 + (n * NG + h + 1))
                        dve.sem_inc(carrier["dve"], 1)
                        v.tensor_copy(AT[h][:, 0:GROUP], tiles_of(src, i * 2 + h)).then_inc(staged, 1)
                dve.wait_ge(proj_out, (n + 1) * NG + 2)

            def pick(g):
                cf = [a.rearrange("p r c e -> p (r c e)") for a in (cand, cidx, cbase, pos)]
                kf = keys.rearrange("p r k -> p (r k)")
                pk.mark(v.tensor_tensor(kf, cf[1], cf[2], ALU.add))
                pk.mark(v.tensor_scalar(cf[3], cf[0], 0.0, None, ALU.is_gt))
                pk.mark(v.tensor_reduce(s4[:, 0, :], cand[:, :, :, 7], AX.X, ALU.max))
                pk.settle()
                pk.mark(v.tensor_tensor(kf, kf, cf[3], ALU.mult))
                pk.mark(v.tensor_reduce(s4[:, 1, :], pos.rearrange("p r c e -> p r (c e)"), AX.X, ALU.add))
                for r in range(TPG):
                    pk.mark(v.tensor_tensor_scan(zcum[:, r, :], ones, zero[:, r, :], 0.0, ALU.mult, ALU.add))
                pk.settle()
                pk.mark(v.tensor_scalar(s4[:, 2, :], s4[:, 1, :], -1.0, float(TOPK), ALU.mult, ALU.add))
                for rd in range(ROUNDS):
                    for r in range(TPG):
                        pk.mark(v.max(top[:, r, rd * 8:rd * 8 + 8], keys[:, r, :]))
                    pk.settle()
                    if rd + 1 < ROUNDS:
                        for r in range(TPG):
                            pk.mark(v.match_replace(keys[:, r, :], top[:, r, rd * 8:rd * 8 + 8], keys[:, r, :], 0.0))
                        pk.settle()
                pk.mark(v.tensor_tensor(zcum, zcum, s4[:, 2, :].unsqueeze(2).to_broadcast([P, TPG, PREFIX]), ALU.is_lt))
                pk.mark(v.tensor_scalar(topm, top, 0.0, None, ALU.is_gt))
                pk.mark(v.tensor_scalar(s4[:, 4, :], s4[:, 0, :], 0.0, None, ALU.is_gt))
                pk.settle()
                pk.mark(v.tensor_reduce(s4[:, 3, :], zcum, AX.X, ALU.add))
                pk.mark(v.scalar_tensor_tensor(s4[:, 4, :], s4[:, 1, :], float(TOPK) - 0.5, s4[:, 4, :], ALU.is_gt, ALU.max))
                pk.mark(v.tensor_scalar(s4[:, 5, :], s4[:, 6, :], 0.0, None, ALU.is_lt))
                pk.settle()
                pk.mark(v.tensor_scalar(s4[:, 3, :], s4[:, 3, :], float(N), None, ALU.add))
                pk.mark(v.tensor_tensor(tiles_of(FLAGS[:, 1, :], g), s4[:, 4, :], s4[:, 5, :], ALU.max))
                pk.mark(v.tensor_copy(tiles_of(FLAGS[:, 0, :], g), s4[:, 1, :]))
                pk.settle()
                slot0 = s4[:, 3, :].unsqueeze(2).to_broadcast([P, TPG, TOPK])
                pk.mark(v.scalar_tensor_tensor(topd, top, -1.0, slot0, ALU.add, ALU.subtract))
                pk.settle()
                pk.mark(v.tensor_tensor(topd, topd, topm, ALU.mult))
                pk.settle()
                pk.mark(v.tensor_tensor(tiles_of(IDX[:, :, 1:NGATHER], g), topd[:, :, 0:TOPK - 1],
                                        slot0[:, :, 0:TOPK - 1], ALU.add))
                pk.mark(v.tensor_copy(tiles_of(IDX[:, :, 0], g), s4[:, 3, :]))
                pk.settle()

            def scan_pass():
                with dve.Fori(0, NG) as g:
                    sc.enter(g, SCAN[0] * NPC)
                    pk.enter(g, PICK)
                    for c in range(NPC):
                        dve.wait_ge(piece_loaded[c % SLOTS], g * (16 * K4) + 16 * (c // SLOTS + 1))
                        dve.sem_inc(carrier["dve"], 1)
                        pc = pieces[c % SLOTS]
                        if c == 0:
                            pk.mark(v.tensor_scalar(zero, pc[:, :, 0:PREFIX], 0.0, None, ALU.is_equal))
                            pk.mark(v.tensor_reduce(s4[:, 6, :], pc[:, :, 0:PREFIX], AX.X, ALU.min))
                            pk.settle()
                        found = []
                        for r in range(TPG + 1):
                            if r < TPG:
                                found.append(sc.mark(v.max(cand[:, r, c, :], pc[:, r, :])))
                            if r:
                                sc.settle(found[r - 1])
                                sc.mark(v.max_index(cidx[:, r - 1, c, :], cand[:, r - 1, c, :], pc[:, r - 1, :]))
                    sc.settle()
                    dve.wait_ge(pick_constants, 2)
                    pick(g)
                    dve.wait_ge(piece_summed, g * NPC + (NPC + SLOTS))
                    dve.sem_inc(carrier["dve"], 1)
                    pk.mark(v.tensor_reduce(tiles_of(RS[:, :], g), rs_part[:, :, :], AX.X, ALU.add))
                    pk.settle(tell=rs_reduced)
                sc.leave(NG)
                pk.leave(NG)

            def dot_pass(q):
                dt_ = Steps(dve, piece_scanned[q], carrier["dve"])
                dt_.base = SCAN[q] * SLOTS
                with dve.Fori(0, NG) as g:
                    dt_.enter(g, BPP * NPC)
                    st.enter(g, 3)
                    for c in range(NPC):
                        dve.wait_ge(piece_loaded[c % SLOTS], g * (16 * K4) + 16 * (q * NG * K4 + c // SLOTS + 1))
                        dve.sem_inc(carrier["dve"], 1)
                        for b in range(BPP):
                            piece, scale = pieces_t[c % SLOTS][:, b, :], dots[:, c * BPP + b:c * BPP + b + 1]
                            if c == 0:
                                dt_.mark(v.tensor_scalar(dacc[:, b, :], piece, scale, None, ALU.mult))
                            else:
                                dt_.settle(dt_.k + 1 - BPP)
                                dt_.mark(v.scalar_tensor_tensor(dacc[:, b, :], piece, scale, dacc[:, b, :],
                                                                ALU.mult, ALU.add))
                    dt_.settle()
                    mark(v.tensor_tensor(dacc[:, 0:2, :], dacc[:, 0:2, :], dacc[:, 2:4, :], ALU.add))
                    settle()
                    mark(v.tensor_tensor(dacc[:, 0, :], dacc[:, 0, :], dacc[:, 1, :], ALU.add))
                    settle(tell=dots_summed)
                    dve.wait_ge(den_ready, g + ((q - 1) * NG + 1))
                    dve.sem_inc(carrier["dve"], 1)
                    mark(v.tensor_copy(tiles_of(DEN[:, :], g), psX[:, 0:TPG]))
                    settle(tell=den_step)
                dt_.leave(NG)
                st.leave(NG)
                dve.wait_ge(nat_copied, (q + 1) * NG + 1)

            def general_form():
                STEPS = 3 * ROUNDS
                any_general = dve.value_load(CTL[0:1, 2, 0:1], min_val=0, max_val=1)
                with dve.If(any_general > 0):
                    ge = Steps(dve, general_step, carrier["dve"])
                    with dve.Fori(0, NT) as t:
                        general = dve.value_load(CTL[0:1, 1, bass.ds(t, 1)], min_val=0, max_val=1)
                        dve.wait_ge(row_loaded, t * 16 + 16)
                        dve.sem_inc(carrier["dve"], 1)
                        with dve.If(general > 0):
                            ge.enter(t, STEPS)
                            row = PIECES[:, 0:N]
                            for rd in range(ROUNDS):
                                ge.link(v.max(f8[:, :], row))
                                ge.link(v.max_index(fidx[:, rd * 8:rd * 8 + 8], f8[:, :], row))
                                if rd + 1 < ROUNDS:
                                    ge.link(v.match_replace(row, f8[:, :], row, -3.0e38))
                            ge.mark(v.tensor_copy(IDX[:, bass.ds(t, 1), :], fidx[:, :].unsqueeze(1)))
                            ge.settle(tell=row_used)
                        with dve.Else():
                            dve.sem_inc(general_step, STEPS)
                            dve.sem_inc(row_used, 1)
            dve.sem_inc(den_step, 1)
            link(v.memset(ones_col[:, :], 1.0))

            def reduce_gathers(par, n, cuts):
                def reduce():
                    v.tensor_reduce(gmax[:, :], ring[par][:, 0:cuts[0], :].rearrange("p k f -> p f k"),
                                    AX.X, ALU.max).then_inc(gather_step, 1)
                if len(cuts) == 1:
                    reduce()
                    return
                with dve.If(n < cuts[0] + 1):
                    reduce()
                with dve.Else():
                    reduce_gathers(par, n, cuts[1:])

            def add_expmap(least):
                squares(2)
                link(v.tensor_scalar(S(2), S(2), least, None, ALU.max))
                ask()
                ask()
                link(v.reciprocal(S(2), S(2)))
                link(v.tensor_tensor(S(3), S(3), S(2), ALU.mult))
                link(v.tensor_tensor(AGG[:, :, :], AGG[:, :, :], by_row(S(3)), ALU.mult))
                link(v.tensor_tensor(X[:, :, :], X[:, :, :], AGG[:, :, :], ALU.add))

            def give_pieces(q):
                dve.sem_inc(piece_scanned[q], SCAN[q] * SLOTS)

            sc = Steps(dve, piece_scanned[0], carrier["dve"])
            pk = Steps(dve, pick_step, carrier["dve"])
            give_pieces(0)
            dve.sem_inc(rs_reduced, 1)
            dve.sem_inc(row_used, 1)
            dve.sem_inc(den_step, 1)
            link(v.memset(ones_col[:, :], 1.0))
            sc.base = SCAN[0] * SLOTS
            dve.wait_ge(s_load, LOADS)
            dve.wait_ge(ident_ready, 2)
            link(v.tensor_scalar(alph[:, 1:2], alph[:, 0:1], -1.0, 1.0, ALU.mult, ALU.add))
            layernorm()
            project(0, H)
            dve.sem_inc(pass_ready, 1)
            scan_pass()
            dve.sem_inc(flags_ready, 1)
            dve.wait_ge(nat_copied, NG + 1)
            link(v.tensor_scalar(S(2), RS[:, :], alph[:, 0:1], alph[:, 1:2], ALU.mult, ALU.add))
            link(v.tensor_scalar(S(3), S(2), 0.0, None, ALU.is_equal))
            link(v.tensor_tensor(S(2), S(2), S(3), ALU.add))
            link(v.reciprocal(S(2), S(2)))
            link(v.tensor_scalar(S(3), S(3), -1.0, 1.0, ALU.mult, ALU.add))
            link(v.tensor_tensor(S(2), S(2), S(3), ALU.mult))
            ask()
            link(v.scalar_tensor_tensor(AGG[:, :, :], AGG[:, :, :], alph[:, 0:1], H[:, :, :], ALU.mult, ALU.add))
            link(v.tensor_tensor(AGG[:, :, :], AGG[:, :, :], by_row(S(2)), ALU.mult))
            link(v.tensor_tensor(AGG[:, :, :], AGG[:, :, :], by_feature(0), ALU.add))
            link(v.scalar_tensor_tensor(X[:, :, :], AGG[:, :, :], 0.0, X[:, :, :], ALU.max, ALU.add))

            dve.wait_ge(flags_reduced, 1)
            link(v.tensor_scalar(ctlf[:, 1, :], FLAGR[0:1, 1, :], 0.0, None, ALU.is_gt))
            link(v.tensor_scalar(ctlf[:, 0, :], ctlf[:, 1, :], float(NGATHER), None, ALU.mult))
            link(v.scalar_tensor_tensor(ctlf[:, 0, :], FLAGR[0:1, 0, :], 1.0, ctlf[:, 0, :], ALU.add, ALU.max))
            link(v.tensor_scalar(CTL[:, 0, :], ctlf[:, 0, :], float(NGATHER), None, ALU.min))
            link(v.tensor_copy(CTL[:, 1, :], ctlf[:, 1, :]))
            link(v.tensor_reduce(CTL[:, 2, 0:1], ctlf[:, 1, :], AX.X, ALU.max), tell=ctl_ready)
            general_form()
            give_pieces(1)

            layernorm()
            squares(2)
            dve.wait_ge(turned_stored, 1)
            project(1, H)
            squares(3)
            link(v.tensor_scalar(S(4), S(3), 0.0, None, ALU.add))
            link(v.tensor_scalar(sm[:, 2:4, :], sm[:, 2:4, :], 1e-30, None, ALU.max))
            ask()
            link(v.tensor_scalar(S(5), S(2), 1.0 - 1e-5, None, ALU.min))
            artanh(S(6), S(5))
            link(v.reciprocal(S(7), S(2)))
            link(v.tensor_tensor(S(5), S(3), S(7), ALU.mult))
            link(v.tensor_tensor(S(5), S(5), S(6), ALU.mult))
            ask()
            link(v.reciprocal(S(7), S(3)))
            link(v.tensor_tensor(S(7), S(7), S(5), ALU.mult))
            link(v.tensor_tensor(S(6), S(7), S(7), ALU.mult))
            link(v.tensor_tensor(S(6), S(6), S(4), ALU.mult))
            link(v.tensor_scalar(S(6), S(6), -1.0, 1.0, ALU.mult, ALU.add))
            link(v.tensor_scalar(S(6), S(6), 1e-5, None, ALU.max))
            link(v.reciprocal(S(6), S(6)))
            link(v.tensor_scalar(dots[:, :], S(6), 2.0, -1.0, ALU.mult, ALU.add))
            link(v.scalar_tensor_tensor(S(7), S(6), 2.0, S(7), ALU.mult, ALU.mult))
            link(v.tensor_tensor(H[:, :, :], AGG[:, :, :], by_row(S(7)), ALU.mult), tell=pass_ready)
            dot_pass(1)
            link(v.tensor_scalar(S(5), DEN[:, :], 1e-10, None, ALU.max))
            link(v.tensor_scalar(S(6), DEN[:, :], -1e-10, None, ALU.min))
            link(v.tensor_scalar(S(7), DEN[:, :], 0.0, None, ALU.is_ge))
            link(v.tensor_tensor(S(5), S(5), S(6), ALU.subtract))
            link(v.tensor_tensor(S(5), S(5), S(7), ALU.mult))
            link(v.tensor_tensor(S(5), S(5), S(6), ALU.add))
            link(v.reciprocal(S(8), S(5)))
            squares(2)
            link(v.tensor_tensor(S(2), S(2), S(8), ALU.mult))
            link(v.tensor_tensor(S(2), S(2), S(8), ALU.mult))
            link(v.tensor_scalar(S(2), S(2), 1e-30, None, ALU.max))
            ask()
            link(v.tensor_scalar(S(3), S(2), 1.0 - 1e-5, None, ALU.min))
            artanh(S(4), S(3))
            ask()
            link(v.reciprocal(S(2), S(2)))
            link(v.tensor_tensor(S(8), S(8), S(2), ALU.mult))
            link(v.tensor_scalar(S(5), S(4), 1e-15, None, ALU.max))
            link(v.reciprocal(S(7), S(5)))
            link(v.tensor_tensor(S(4), S(4), S(7), ALU.mult))
            link(v.tensor_scalar(S(3), S(5), 1.0 - 1e-5, None, ALU.min))
            artanh(S(6), S(3))
            link(v.tensor_tensor(S(6), S(6), RS[:, :], ALU.mult))
            ask()
            link(v.tensor_tensor(S(6), S(6), S(4), ALU.mult))
            link(v.tensor_tensor(S(8), S(8), S(6), ALU.mult))
            link(v.tensor_scalar(S(5), S(6), -1.0, None, ALU.mult))
            link(v.tensor_tensor(S(5), S(5), S(6), ALU.max))
            link(v.tensor_scalar(S(5), S(5), 1e-15, None, ALU.max))
            link(v.tensor_scalar(S(3), S(5), 1.0 - 1e-5, None, ALU.min))
            artanh(S(4), S(3))
            link(v.reciprocal(S(5), S(5)))
            link(v.tensor_tensor(S(8), S(8), S(4), ALU.mult))
            link(v.tensor_tensor(S(8), S(8), S(5), ALU.mult))
            link(v.tensor_tensor(AGG[:, :, :], AGG[:, :, :], by_row(S(8)), ALU.mult))
            link(v.tensor_scalar(AGG[:, :, :], AGG[:, :, :], 0.0, None, ALU.max))
            add_expmap(1e-30)

            layernorm()
            project(2, H)
            link(v.tensor_tensor(AGG[:, :, :], AGG[:, :, :], by_feature(1), ALU.add), tell=h_ready)
            dve.wait_ge(prefix_copied, 1)
            link(v.tensor_tensor_scan(pfx[:, 1, :], pfx[:, 0, :], pfx[:, 0, :], -3.0e38, ALU.max, ALU.max),
                 tell=prefix_scanned)
            gr = Steps(dve, gather_step, carrier["dve"])
            for par in range(2):
                gr.link(v.tensor_copy(idx_now[par][:, :], IDX[:, par, :]), tell=idx_staged)
            with dve.Fori(0, NT // 2) as i:
                gr.enter(i, 6)
                for par in range(2):
                    n = dve.value_load(CTL[0:1, 0, bass.ds(i * 2 + par, 1)], min_val=1, max_val=NGATHER)
                    dve.wait_ge(gathered[par], i * FULL + FULL)
                    dve.sem_inc(carrier["dve"], 1)
                    reduce_gathers(par, n, CUTS)
                    gr.k += 1
                    gr.settle()
                    t = i * 2 + par
                    gr.mark(v.tensor_tensor(X[:, bass.ds(t, 1), :], X[:, bass.ds(t, 1), :],
                                            gmax[:, :].unsqueeze(1), ALU.add))
                    gr.mark(v.tensor_copy(idx_now[par][:, :], IDX[:, bass.ds(t + 2, 1), :]))
                    gr.settle(tell=idx_staged)
            gr.leave(NT // 2)
            give_pieces(2)

            layernorm()
            squares(2)
            link(v.tensor_scalar(S(2), S(2), -1.0, 1.0, ALU.mult, ALU.add))
            link(v.reciprocal(S(2), S(2)))
            link(v.tensor_scalar(S(7), S(2), 2.0, 1e7, ALU.mult, ALU.min))
            link(v.tensor_scalar(S(3), RS[:, :], 1.0, None, ALU.add))
            ask()
            link(v.reciprocal(dots[:, :], S(3)))
            link(v.tensor_tensor(H[:, :, :], H[:, :, :], by_row(dots[:, :]), ALU.mult), tell=pass_ready)
            dot_pass(2)
            link(v.tensor_tensor(S(5), DEN[:, :], dots[:, :], ALU.add))
            link(v.scalar_tensor_tensor(S(5), S(7), -1.0, S(5), ALU.add, ALU.mult))
            link(v.reciprocal(S(5), S(5)))
            link(v.tensor_tensor(S(5), S(5), S(7), ALU.mult))
            link(v.tensor_tensor(AGG[:, :, :], AGG[:, :, :], H[:, :, :], ALU.add))
            link(v.tensor_tensor(AGG[:, :, :], AGG[:, :, :], by_row(S(5)), ALU.mult))
            squares(2)
            link(v.tensor_scalar(S(2), S(2), 1e-30, None, ALU.max))
            ask()
            link(v.tensor_scalar(S(3), S(2), 1e-7, 1.0 - 1e-7, ALU.max, ALU.min))
            artanh(S(4), S(3))
            ask()
            link(v.reciprocal(S(5), S(3)))
            link(v.tensor_tensor(S(8), S(4), S(5), ALU.mult))
            link(v.tensor_tensor(S(3), S(2), S(8), ALU.mult))
            link(v.tensor_scalar(S(3), S(3), 1e-7, 1.0 - 1e-7, ALU.max, ALU.min))
            artanh(S(4), S(3))
            link(v.reciprocal(S(3), S(3)))
            link(v.tensor_tensor(S(8), S(8), S(4), ALU.mult))
            link(v.tensor_tensor(S(8), S(8), S(3), ALU.mult))
            link(v.tensor_tensor(H[:, :, :], AGG[:, :, :], by_row(S(8)), ALU.mult))
            project(3, H)
            link(v.tensor_tensor(AGG[:, :, :], AGG[:, :, :], by_feature(2), ALU.add))
            link(v.tensor_scalar(AGG[:, :, :], AGG[:, :, :], 0.0, None, ALU.max))
            add_expmap(1e-14)
            dve.sem_inc(x_done, 1)


_INS = ["x", "adj", "L0_gnn_alpha", "L0_gnn_W", "L0_gnn_b", "L1_gnn_W", "L2_gnn_W", "L2_gnn_b", "L3_gnn_W",
        "L3_gnn_b"]


def kernel(**inputs):
    import numpy as np
    import concourse.bacc as bacc
    from concourse.bass_utils import run_bass_kernel_spmd

    nc = bacc.Bacc("TRN2", target_bir_lowering=False, num_devices=1)
    arrays, args = {}, []
    for name in _INS:
        a = np.ascontiguousarray(inputs[name])
        arrays[f"in_{name}"] = a
        args.append(nc.dram_tensor(f"in_{name}", a.shape, mybir.dt.from_np(a.dtype), kind="ExternalInput").ap())
    out = nc.dram_tensor("out_x", inputs["x"].shape, mybir.dt.float32, kind="ExternalOutput").ap()
    build(nc, *args, out)
    r = run_bass_kernel_spmd(nc, [arrays], core_ids=[0])
    return r.results[0]["out_x"]
```

```python
import concourse.bass as bass
from concourse import mybir
from contextlib import ExitStack

P = 128
TPG = 4
GROUP = TPG * P
PIECE = 512
SLOTS = 4
TOPK = 32
PREFIX = 64
NGATHER = TOPK
COMMON = 14
CUTS = [16, 17, 18, 19, 20, 21, 23, 26, NGATHER]
ROUNDS = TOPK // 8
NAT = 4
CT = 4
LN_EPS = 1e-5

fp32 = mybir.dt.float32
u32 = mybir.dt.uint32
i32 = mybir.dt.int32
ALU = mybir.AluOpType
ACT = mybir.ActivationFunctionType
AX = mybir.AxisListType
RMAX = bass.bass_isa.ReduceOp.max


class Steps:

    def __init__(self, engine, semaphore, carrier):
        self.engine, self.semaphore, self.carrier = engine, semaphore, carrier
        self.base, self.turn, self.per, self.k = 0, None, 0, 0

    def value(self, k):
        return self.base + k if self.turn is None else self.turn * self.per + (self.base + k)

    def mark(self, instruction):
        instruction.then_inc(self.semaphore, 1)
        self.k += 1
        return self.k

    def settle(self, k=None, tell=None):
        self.engine.wait_ge(self.semaphore, self.value(self.k if k is None else k))
        if tell is not None:
            self.engine.sem_inc(tell, 1)
        elif self.turn is not None:
            self.engine.sem_inc(self.carrier, 1)

    def link(self, instruction, tell=None):
        self.mark(instruction)
        self.settle(tell=tell)

    def enter(self, turn, per):
        self.base, self.turn, self.per, self.k = self.base + self.k, turn, per, 0

    def leave(self, turns):
        assert self.k == self.per, (self.k, self.per)
        self.base, self.turn, self.k = self.base + turns * self.per, None, 0


def build(nc, x, adj, alpha, w0, b0, w1, w2, b2, w3, b3, out):
    N = x.shape[0]
    NT = N // P
    NG = NT // TPG
    NPC = N // PIECE
    BPP = PIECE // P
    NP = NT // 2
    K4 = NPC // SLOTS
    CHUNKS = NT // CT
    GB = 2 * NG // CT
    PPC = CT // BPP
    EB = CT // 4
    assert NG % 2 == 0 and NPC % SLOTS == 0 and CT == BPP and GB * PPC % SLOTS == 0

    x_v = x.rearrange("(t p) f -> p t f", p=P)
    out_v = out.rearrange("(t p) f -> p t f", p=P)
    adj_v = adj.rearrange("(g r p) (c x) -> g c p r x", p=P, r=TPG, x=PIECE)
    adj_rows = adj.rearrange("(t p) n -> t p n", p=P)
    table = nc.dram_tensor("h_table", (N + PREFIX, P), fp32).ap()
    turned = nc.dram_tensor("adj_turned", (NG, NP, P, 2 * GROUP), fp32).ap()
    turned_v = turned.rearrange("g (c k) p x -> g c p k x", k=2)

    h3 = nc.dram_tensor("h3_rows", (N, P), fp32).ap().rearrange("(t p) f -> p t f", p=P)

    ctx = ExitStack()
    with ctx:
        def sb(name, shape, dt=fp32):
            return ctx.enter_context(nc.sbuf_tensor(name, shape, dt))

        def pb(name, shape):
            return ctx.enter_context(nc.psum_tensor(name, shape, fp32))

        def sem(name):
            return ctx.enter_context(nc.semaphore(name))

        X = sb("X", [P, NT, P])
        H = sb("H", [P, NT, P])
        AGG = sb("AGG", [P, NT, P])
        D = sb("D", [P, max(N, 2 * NGATHER * P)])
        PIECES = sb("PIECES", [P, max(SLOTS * TPG * PIECE, N)])
        ATS = sb("ATS", [P, NAT, 2 * GROUP])
        AT = [ATS[:, i, :] for i in range(NAT)]
        aggT = sb("aggT", [P, GROUP])
        gmax = sb("gmax", [P, P])
        ident = sb("ident", [P, P])
        wnat = sb("wnat", [P, 2, P])
        W = [sb(f"W{i}", [P, P]) for i in range(4)]
        bias = sb("bias", [P, 3, P])
        alph = sb("alph", [P, 2])
        IDX = sb("IDX", [P, NT + 2, NGATHER], mybir.dt.uint16)
        idx_now = [sb(f"idx_now{i}", [P, NGATHER], u32) for i in range(2)]
        rs_part = sb("rs_part", [P, TPG, NPC])
        RS = sb("RS", [P, NT])
        DEN = sb("DEN", [P, NT])
        FLAGS = sb("FLAGS", [P, 2, NT])
        FLAGR = sb("FLAGR", [P, 2, NT])
        CTL = sb("CTL", [1, 3, NT], i32)
        ctlf = sb("ctlf", [1, 2, NT])
        sm = sb("sm", [P, 14, NT])
        dots = sb("dots", [P, NT])
        DINV = sb("DINV", [P, NT])
        R2 = sb("R2", [P, NT])
        DEN3 = sb("DEN3", [P, NT])
        ones_col = sb("ones_col", [P, 1])
        s4 = sb("s4", [P, 10, TPG])
        f8 = sb("f8", [P, 8])
        fidx = sb("fidx", [P, TOPK], u32)
        pfx = sb("pfx", [P, 2, PREFIX])
        pfxn = sb("pfxn", [PREFIX, P])
        xc = sb("xc", [P, 2, P])
        tsc = sb("tsc", [P, 2, 4])
        eps_col = sb("eps_col", [P, 1])

        pieces = [PIECES[:, i * TPG * PIECE:(i + 1) * TPG * PIECE].rearrange("p (r x) -> p r x", r=TPG)
                  for i in range(SLOTS)]
        SQ = D[:, 0:N].rearrange("p (t f) -> p t f", f=P)
        pieces_t = [PIECES[:, i * TPG * PIECE:(i + 1) * TPG * PIECE].rearrange("p (b x) -> p b x", b=BPP)
                    for i in range(SLOTS)]
        ring = [D[:, i * NGATHER * P:(i + 1) * NGATHER * P].rearrange("p (k f) -> p k f", f=P) for i in range(2)]
        dacc = ATS[:, 0:2, :].rearrange("p k (b x) -> p (k b) x", b=2)
        sum1 = [D[:, i * GROUP:(i + 1) * GROUP] for i in range(2)]
        dot1 = [[D[:, (2 + 2 * k + i) * GROUP:(3 + 2 * k + i) * GROUP] for i in range(2)] for k in range(2)]
        dacc3 = D[:, 6 * GROUP:(6 + EB) * GROUP].rearrange("p (b x) -> p b x", b=EB)
        Hc = [ATS[:, i, 0:CT * P].rearrange("p (t f) -> p t f", f=P) for i in range(2)]
        ACC = AGG[:, :, :].rearrange("p (g r) f -> p g (r f)", r=TPG)
        DOT = H[:, :, :].rearrange("p (g r) f -> p g (r f)", r=TPG)
        CW = NPC * 8
        at = [0]

        def part(n):
            at[0] += n
            assert at[0] <= D.shape[1]
            return D[:, at[0] - n:at[0]]

        cand = part(TPG * CW).rearrange("p (r c e) -> p r c e", r=TPG, e=8)
        cidx = part(TPG * CW).bitcast(u32).rearrange("p (r c e) -> p r c e", r=TPG, e=8)
        cbase = part(TPG * CW).rearrange("p (r c e) -> p r c e", r=TPG, e=8)
        pos = part(TPG * CW).rearrange("p (r c e) -> p r c e", r=TPG, e=8)
        keys = part(TPG * CW).rearrange("p (r k) -> p r k", r=TPG)
        zero = part(TPG * PREFIX).rearrange("p (r k) -> p r k", r=TPG)
        zcum = part(TPG * PREFIX).rearrange("p (r k) -> p r k", r=TPG)
        ones = part(PREFIX)
        top = part(TPG * TOPK).rearrange("p (r k) -> p r k", r=TPG)
        topm = part(TPG * TOPK).rearrange("p (r k) -> p r k", r=TPG)
        topd = part(TPG * TOPK).rearrange("p (r k) -> p r k", r=TPG)

        psT = [pb(f"psT{i}", [P, 2 * GROUP]) for i in range(2)]
        psA = pb("psA", [P, GROUP])
        psN = pb("psN", [P, GROUP])
        psX = pb("psX", [P, GROUP])
        psY = pb("psY", [P, GROUP])
        acc = [psA[:, :], psY[:, :]]
        acc3 = [psT[k][:, h * GROUP:(h + 1) * GROUP] for k in range(2) for h in range(2)]
        junk = [psX, psY]

        s_load = sem("s_load")
        s_ident = sem("s_ident")
        ident_ready = sem("ident_ready")
        pick_constants = sem("pick_constants")
        prefix_copied = sem("prefix_copied")
        weights_transposed = sem("weights_transposed")
        carrier = {e: sem(f"carrier_{e}") for e in ("dve", "act", "pe", "sp", "pool")}
        dve_step = sem("dve_step")
        pick_step = sem("pick_step")
        act_step = sem("act_step")
        piece_loaded = [sem(f"piece_loaded{i}") for i in range(SLOTS)]
        pass_ready = sem("pass_ready")
        pair_transposed = sem("pair_transposed")
        piece_scanned = [sem(f"piece_scanned{q}") for q in range(3)]
        piece_summed = sem("piece_summed")
        pair_copied = sem("pair_copied")
        pair_used = sem("pair_used")
        acc_copied = sem("acc_copied")
        nat_ready = sem("nat_ready")
        nat_copied = sem("nat_copied")
        rs_reduced = sem("rs_reduced")
        flags_ready = sem("flags_ready")
        flags_reduced = sem("flags_reduced")
        ctl_ready = sem("ctl_ready")
        row_loaded = sem("row_loaded")
        row_used = sem("row_used")
        general_step = sem("general_step")
        for_act = sem("for_act")
        from_act = sem("from_act")
        staged = sem("staged")
        stage_read = sem("stage_read")
        hT_copied = sem("hT_copied")
        projected = sem("projected")
        proj_out = sem("proj_out")
        pair_stored = [sem(f"pair_stored{i}") for i in range(NAT)]
        pair_free = sem("pair_free")
        turned_stored = sem("turned_stored")
        piece_multiplied = [sem(f"piece_multiplied{q}") for q in (1, 2)]
        dots_summed = sem("dots_summed")
        squared = sem("squared")
        sums_squared = sem("sums_squared")
        own_added = sem("own_added")
        prefix_t = sem("prefix_t")
        prefix_scanned = sem("prefix_scanned")
        prefix_n = sem("prefix_n")
        prefix_ready = sem("prefix_ready")
        table_stored = sem("table_stored")
        idx_staged = sem("idx_staged")
        gathered = [sem(f"gathered{i}") for i in range(2)]
        gather_step = sem("gather_step")
        centered = sem("centered")
        rooted = sem("rooted")
        scaled = sem("scaled")
        tiles_made = sem("tiles_made")
        h3_stored = [sem(f"h3_stored{i}") for i in range(2)]
        h3_loaded = sem("h3_loaded")
        sums_added = sem("sums_added")
        ring_done = sem("ring_done")
        x_done = sem("x_done")
        s_out = sem("s_out")

        block = ctx.enter_context(nc.Block())
        LOADS = 9 * 16
        HALF = [slice(0, NT // 2), slice(NT // 2, NT)]
        STORES = 5 * 16
        PICK = 22 + 2 * ROUNDS * TPG
        SCAN = 2 * TPG
        TAKES1 = [BPP + (EB if h == PPC - 1 else 0) for h in range(PPC)] * CHUNKS
        TAKES3 = [BPP - (EB if h == PPC - 1 else 0) for h in range(PPC)] * GB

        def scanned_before(takes, k):
            return sum(takes) + sum(takes[:k - SLOTS + 1]) if k >= SLOTS else sum(takes[:len(takes) + k - SLOTS + 1])
        FULL = 16 * NGATHER

        def tiles_of(A, g):
            return A[:, bass.ds(g * TPG, TPG)]

        def chunk_piece(c, i, m, h):
            k = m * PPC + h
            turns = GB * PPC // SLOTS
            return (i * (GB * PPC) + (c * NG * PPC + k), k % SLOTS,
                    i * (16 * turns) + 16 * (2 * NG * K4 + c * (CT // 2) * turns + k // SLOTS + 1))

        @block.sync
        def _(sp):
            sp.dma_start(X[:, :, :], x_v).then_inc(s_load, 16)
            sp.dma_start(wnat[:, 0, :], w0).then_inc(s_load, 16)
            sp.dma_start(wnat[:, 1, :], w2).then_inc(s_load, 16)
            sp.dma_start(W[1][:, :], w1).then_inc(s_load, 16)
            sp.dma_start(W[3][:, :], w3).then_inc(s_load, 16)
            for n, b in enumerate((b0, b2, b3)):
                sp.dma_start(bias[:, n, :], b.partition_broadcast(P)).then_inc(s_load, 16)
            sp.dma_start(alph[:, 0:1], alpha.partition_broadcast(P)).then_inc(s_load, 16)

            def load_pieces():
                with sp.Fori(0, NG) as g:
                    for c in range(NPC):
                        sp.wait_ge(pair_transposed, g * (2 * NPC) + 2 * (c + 1))
                        sp.sem_inc(carrier["sp"], 1)
                        sp.wait_ge(piece_scanned[0], g * (NPC * SCAN) + SCAN * (c + 1))
                        sp.sem_inc(carrier["sp"], 1)
                        sp.wait_ge(piece_summed, g * NPC + (c + 1))
                        sp.sem_inc(carrier["sp"], 1)
                        sp.dma_start(pieces[c % SLOTS], adj_v[bass.ds(g, 1), c, :, :, :])\
                          .then_inc(piece_loaded[c % SLOTS], 16)

            def load_turned():
                with sp.Fori(0, NG) as g:
                    for c in range(NPC):
                        sp.wait_ge(piece_multiplied[0], g * NPC + (c + 1))
                        sp.sem_inc(carrier["sp"], 1)
                        sp.wait_ge(piece_scanned[1], g * sum(TAKES1) + scanned_before(TAKES1, c))
                        sp.sem_inc(carrier["sp"], 1)
                        sp.dma_start(PIECES[:, (c % SLOTS) * TPG * PIECE:(c % SLOTS + 1) * TPG * PIECE]
                                     .rearrange("p (k x) -> p k x", k=2), turned_v[bass.ds(g, 1), c, :, :, :])\
                          .then_inc(piece_loaded[c % SLOTS], 16)

            load_pieces()

            sp.wait_ge(ctl_ready, 1)
            any_general = sp.value_load(CTL[0:1, 2, 0:1], min_val=0, max_val=1)
            with sp.If(any_general > 0):
                with sp.Fori(0, NT) as t:
                    general = sp.value_load(CTL[0:1, 1, bass.ds(t, 1)], min_val=0, max_val=1)
                    sp.wait_ge(row_used, t + 1)
                    sp.sem_inc(carrier["sp"], 1)
                    with sp.If(general > 0):
                        sp.dma_start(PIECES[:, 0:N], adj_rows[bass.ds(t, 1), :, :]).then_inc(row_loaded, 16)
                    with sp.Else():
                        sp.dma_start(PIECES[0:16, 0:8], adj_rows[0, 0:16, 0:8]).then_inc(row_loaded, 16)

            sp.wait_ge(turned_stored, 1)
            load_turned()

            table_v = table[0:N, :].rearrange("(t p) f -> p t f", p=P)
            for k in range(4):
                sp.wait_ge(proj_out, 2 * NG + 2 + (k + 1) * (NG // 4))
                quarter = slice(k * (NT // 4), (k + 1) * (NT // 4))
                sp.dma_start(table_v[:, quarter, :], AGG[:, quarter, :]).then_inc(table_stored, 16)
            sp.wait_ge(prefix_ready, 1)
            sp.dma_start(table[N:N + PREFIX, :], pfxn[:, :]).then_inc(table_stored, 16)

            for c in range(CHUNKS):
                with sp.Fori(0, CT // 2) as i:
                    for m in range(GB):
                        for h in range(PPC):
                            n, slot, _ = chunk_piece(c, i, m, h)
                            sp.wait_ge(piece_multiplied[1], n + 1)
                            sp.sem_inc(carrier["sp"], 1)
                            sp.wait_ge(piece_scanned[2], i * sum(TAKES3) +
                                       (c * (CT // 2) * sum(TAKES3) + scanned_before(TAKES3, (m | 1) * PPC + h)))
                            sp.sem_inc(carrier["sp"], 1)
                            sp.dma_start(PIECES[:, slot * TPG * PIECE:(slot + 1) * TPG * PIECE]
                                         .rearrange("p (k x) -> p k x", k=2),
                                         turned_v[bass.ds(i * GB + m, 1), c * PPC + h, :, :, :])\
                              .then_inc(piece_loaded[slot], 16)

            for k in range(2):
                sp.wait_ge(x_done, k + 1)
                sp.dma_start(out_v[:, HALF[k], :], X[:, HALF[k], :]).then_inc(s_out, 16)
            sp.wait_ge(s_out, 32)
            sp.wait_ge(table_stored, STORES)

        @block.gpsimd
        def _(pool):
            pool.memset(ident[:, :], 0.0).then_inc(s_ident, 1)
            pool.wait_ge(s_ident, 1)
            pool.affine_select(out=ident[:, :], in_=ident[:, :], compare_op=ALU.not_equal, fill=1.0,
                               base=0, pattern=[[-1, P]], channel_multiplier=1).then_inc(ident_ready, 1)
            pool.memset(IDX[:, NT:NT + 2, :], 0).then_inc(ident_ready, 1)
            pool.wait_ge(pass_ready, 1)
            pool.memset(ones, 1.0).then_inc(pick_constants, 1)
            pool.iota(cbase, [[0, TPG], [PIECE, NPC], [0, 8]], base=1, channel_multiplier=0,
                      allow_small_or_imprecise_dtypes=True).then_inc(pick_constants, 1)

            pool.sem_inc(pair_free, NAT)
            with pool.Fori(0, NG) as g:
                def landed(k):
                    pool.wait_ge(pair_stored[k % NAT], g * (16 * (NP // NAT)) + 16 * (k // NAT + 1))
                    pool.sem_inc(pair_free, 1)

                for k in range(NP):
                    pool.wait_ge(pair_copied, g * NP + (k + 1 + 2))
                    pool.sem_inc(carrier["pool"], 1)
                    pool.dma_start(turned[bass.ds(g, 1), k, :, :], AT[k % NAT]).then_inc(pair_stored[k % NAT], 16)
                    if k >= 2:
                        landed(k - 2)
                landed(NP - 2)
                landed(NP - 1)
            pool.sem_inc(turned_stored, 1)

            pool.wait_ge(flags_ready, 1)
            pool.partition_all_reduce(FLAGR[:, :, :].rearrange("p a t -> p (a t)"),
                                      FLAGS[:, :, :].rearrange("p a t -> p (a t)"), P, RMAX)\
                .then_inc(flags_reduced, 1)

            def gather(par, k, inc):
                pool.indirect_dma_start(ring[par][:, k, :], None, table,
                                        bass.IndirectOffsetOnAxis(ap=idx_now[par][:, k:k + 1], axis=0))\
                    .then_inc(gathered[par], inc)

            def gathers(par, n, cuts):
                def leaf(count):
                    for k in range(COMMON, count):
                        share = (NGATHER - COMMON) * (k + 1 - COMMON) // (count - COMMON) - \
                            (NGATHER - COMMON) * (k - COMMON) // (count - COMMON)
                        gather(par, k, 16 * share)
                if len(cuts) == 1:
                    leaf(cuts[0])
                    return
                with pool.If(n < cuts[0] + 1):
                    leaf(cuts[0])
                with pool.Else():
                    gathers(par, n, cuts[1:])

            pool.wait_ge(ctl_ready, 1)
            pool.wait_ge(table_stored, STORES)
            with pool.Fori(0, NT // 2) as i:
                for par in range(2):
                    n = pool.value_load(CTL[0:1, 0, bass.ds(i * 2 + par, 1)], min_val=1, max_val=NGATHER)
                    pool.wait_ge(idx_staged, i * 2 + (par + 1))
                    pool.sem_inc(carrier["pool"], 1)
                    for k in range(COMMON):
                        gather(par, k, 16)
                    gathers(par, n, CUTS)

        @block.tensor
        def _(pe):
            pe.wait_ge(s_load, LOADS)
            pe.wait_ge(ident_ready, 2)
            nc.tensor.transpose(psX[:, 0:P], wnat[:, 0, :], ident[:, :])
            nc.tensor.transpose(psX[:, P:2 * P], wnat[:, 1, :], ident[:, :]).then_inc(weights_transposed, 1)

            def project(n, w):
                with pe.Fori(0, NG // 2) as i:
                    for h in range(2):
                        pe.wait_ge(staged, i * 2 + (n * NG + h + 1))
                        for r in range(TPG):
                            last = nc.tensor.transpose(psT[h][:, r * P:(r + 1) * P],
                                                       AT[h][:, r * P:(r + 1) * P], ident[:, :])
                        last.then_inc(stage_read, 1)
                    for h, ps in enumerate((psX, psY)):
                        pe.wait_ge(hT_copied, i * 2 + (n * NG + h + 1))
                        pe.wait_ge(proj_out, i * 2 + (n * NG + h + 1))
                        for r in range(TPG):
                            last = nc.tensor.matmul(ps[:, r * P:(r + 1) * P],
                                                    AT[h][:, GROUP + r * P:GROUP + (r + 1) * P], W[w][:, :],
                                                    start=True, stop=True)
                        last.then_inc(projected, 1)

            def turn_back(g):
                pe.wait_ge(acc_copied, g + 2)
                pe.wait_ge(nat_copied, g + 1)
                for r in range(TPG):
                    last = nc.tensor.transpose(psN[:, r * P:(r + 1) * P], aggT[:, r * P:(r + 1) * P], ident[:, :])
                last.then_inc(nat_ready, 1)

            def turned_pass():
                def finish(g, p):
                    pe.wait_ge(dots_summed, g + 1)
                    pe.wait_ge(acc_copied, g + (NG + 2))
                    pe.wait_ge(nat_copied, g + (NG + 1))
                    for k in range(2):
                        for r in range(TPG):
                            nc.tensor.matmul(psX[:, bass.ds(g * TPG + (k * NT + r), 1)],
                                             dot1[k][p][:, r * P:(r + 1) * P], ones_col[:, :], start=True, stop=True)
                    for r in range(TPG):
                        last = nc.tensor.transpose(psN[:, r * P:(r + 1) * P], sum1[p][:, r * P:(r + 1) * P],
                                                   ident[:, :])
                    last.then_inc(nat_ready, 1)

                pe.wait_ge(pass_ready, 2)
                with pe.Fori(0, NG // 4) as i:
                    for m in range(4):
                        g = i * 4 + m
                        for c in range(NPC):
                            pe.wait_ge(piece_loaded[c % SLOTS],
                                       i * (64 * K4) + 16 * ((NG + m) * K4 + c // SLOTS + 1))
                            if c == 0:
                                pe.wait_ge(acc_copied, i * 4 + (m + NG))
                            for b in range(BPP):
                                j = BPP * c + b
                                last = nc.tensor.matmul(acc[m % 2], H[:, j, :], pieces_t[c % SLOTS][:, b, :],
                                                        start=(j == 0), stop=(j == NT - 1))
                            last.then_inc(piece_multiplied[0], 1)
                            if c == 1 and m:
                                finish(i * 4 + (m - 1), (m - 1) % 2)
                    finish(i * 4 + 3, 1)

            def adjacency_pass():
                pe.wait_ge(pass_ready, 1)
                with pe.Fori(0, NG) as g:
                    def turn_pair(k):
                        if k % 2 == 0:
                            c = k // 2
                            pe.wait_ge(piece_loaded[c % SLOTS], g * (16 * K4) + 16 * (c // SLOTS + 1))
                        pe.wait_ge(pair_copied, g * NP + (k + 1))
                        for b in range(2):
                            x0 = (k % 2) * 2 * P + b * P
                            for r in range(TPG):
                                last = nc.tensor.transpose(psT[k % 2][:, b * GROUP + r * P:b * GROUP + (r + 1) * P],
                                                           pieces[(k // 2) % SLOTS][:, r, x0:x0 + P], ident[:, :])
                        last.then_inc(pair_transposed, 1)

                    turn_pair(0)
                    for k in range(NP):
                        if k + 1 < NP:
                            turn_pair(k + 1)
                        pe.wait_ge(pair_copied, g * NP + (k + 3))
                        if k == 0:
                            pe.wait_ge(acc_copied, g + 1)
                        for b in range(2):
                            j = 2 * k + b
                            last = nc.tensor.matmul(psA[:, :], H[:, j, :], AT[k % NAT][:, b * GROUP:(b + 1) * GROUP],
                                                    start=(j == 0), stop=(j == NT - 1))
                        last.then_inc(pair_used, 1)
                    turn_back(g)

            def chunk_products():
                def finish(g):
                    pe.wait_ge(sums_added, (CHUNKS - 1) * NG + g + 5)
                    pe.wait_ge(nat_copied, 2 * NG + g + 1)
                    for r in range(TPG):
                        nc.tensor.matmul(psX[:, g * TPG + r:g * TPG + r + 1], DOT[:, g, r * P:(r + 1) * P],
                                         ones_col[:, :], start=True, stop=True)
                    for r in range(TPG):
                        last = nc.tensor.transpose(psN[:, r * P:(r + 1) * P], ACC[:, g, r * P:(r + 1) * P],
                                                   ident[:, :])
                    last.then_inc(nat_ready, 1)

                def products(c, i, m):
                    pe.wait_ge(sums_added, i * GB + (c * NG + m + 1))
                    for h in range(PPC):
                        _, slot, loaded = chunk_piece(c, i, m, h)
                        pe.wait_ge(piece_loaded[slot], loaded)
                        for b in range(BPP):
                            j = h * BPP + b
                            last = nc.tensor.matmul(acc3[m % 4], Hc[c % 2][:, j, :], pieces_t[slot][:, b, :],
                                                    start=(j == 0), stop=(j == CT - 1))
                        last.then_inc(piece_multiplied[1], 1)

                for c in range(CHUNKS):
                    pe.wait_ge(tiles_made, (c + 1) * CT + 2)
                    if c < CHUNKS - 1:
                        with pe.Fori(0, CT // 2) as i:
                            for m in range(GB):
                                products(c, i, m)
                for g in range(NG):
                    products(CHUNKS - 1, g // GB, g % GB)
                    if g >= 2:
                        finish(g - 2)
                for g in (NG - 2, NG - 1):
                    finish(g)

            pe.sem_inc(pair_transposed, 2 * SLOTS)
            pe.sem_inc(pair_used, NAT)
            pe.sem_inc(piece_multiplied[0], SLOTS)
            pe.sem_inc(stage_read, 2)
            pe.sem_inc(nat_ready, 1)
            pe.sem_inc(projected, 2)
            project(0, 0)
            adjacency_pass()
            project(1, 1)
            turned_pass()
            pe.sem_inc(piece_multiplied[1], SLOTS)
            project(2, 2)
            pe.wait_ge(proj_out, 3 * NG + 2)
            nc.tensor.transpose(psX[:, 0:PREFIX], AGG[0:PREFIX, 0, :], ident[0:PREFIX, 0:PREFIX]).then_inc(prefix_t, 1)
            pe.wait_ge(prefix_scanned, 1)
            nc.tensor.transpose(psY[0:PREFIX, 0:P], pfx[:, 1, :], ident[:, :]).then_inc(prefix_n, 1)
            chunk_products()
            project(3, 3)

        @block.scalar
        def _(act):
            st = Steps(act, act_step, carrier["act"])
            asked = [0]

            def job(out, in_, func, **kw):
                asked[0] += 1
                act.wait_ge(for_act, asked[0])
                nc.scalar.activation(out, in_, func, **kw).then_inc(from_act, 1)

            def project(n):
                with act.Fori(0, NG // 2) as i:
                    for h in range(2):
                        act.wait_ge(stage_read, i * 2 + (n * NG + h + 1 + 2))
                        act.wait_ge(projected, i * 2 + (n * NG + h + 1))
                        act.sem_inc(carrier["act"], 1)
                        nc.scalar.activation(AT[h][:, GROUP:2 * GROUP], psT[h][:, 0:GROUP], ACT.Copy)\
                            .then_inc(hT_copied, 1)

            def adjacency_pass():
                with act.Fori(0, NG) as g:
                    st.enter(g, TPG * NPC)
                    for k in range(NP):
                        act.wait_ge(pair_transposed, g * NP + (k + 1 + 2 * SLOTS))
                        act.wait_ge(pair_used, g * NP + (k + 1))
                        act.wait_ge(pair_free, g * NP + (k + 1))
                        nc.scalar.activation(AT[k % NAT], psT[k % 2][:, :], ACT.Copy).then_inc(pair_copied, 1)
                        if k % 2 == 1:
                            c = k // 2
                            if c == 0:
                                act.wait_ge(rs_reduced, g + 1)
                                act.sem_inc(carrier["act"], 1)
                            act.wait_ge(piece_loaded[c % SLOTS], g * (16 * K4) + 16 * (c // SLOTS + 1))
                            act.sem_inc(carrier["act"], 1)
                            for r in range(TPG):
                                if r >= 2:
                                    st.settle(st.k - 1)
                                st.mark(nc.scalar.activation(junk[r % 2][:, :], pieces[c % SLOTS][:, r, :], ACT.Copy,
                                                             accum_out=rs_part[:, r, c:c + 1]))
                            st.settle(tell=piece_summed)
                    act.wait_ge(pair_used, g * NP + (NP + NAT))
                    act.sem_inc(carrier["act"], 1)
                    copy_sums(g)
                st.leave(NG)

            def copy_sums(g):
                act.wait_ge(nat_ready, g + 1)
                act.sem_inc(carrier["act"], 1)
                nc.scalar.activation(aggT[:, :], psA[:, :], ACT.Copy, scale=alph[:, 0:1]).then_inc(acc_copied, 1)
                act.wait_ge(nat_ready, g + 2)
                act.sem_inc(carrier["act"], 1)
                nc.scalar.activation(tiles_of(AGG, g), psN[:, :], ACT.Copy).then_inc(nat_copied, 1)

            def turned_pass():
                with act.Fori(0, NG // 4) as i:
                    st.enter(i, 4 * TPG)
                    for m in range(4):
                        act.wait_ge(piece_multiplied[0], i * (4 * NPC) + ((m + 1) * NPC + SLOTS))
                        act.wait_ge(nat_ready, i * 4 + (m + NG))
                        nc.scalar.activation(sum1[m % 2], acc[m % 2], ACT.Copy).then_inc(acc_copied, 1)
                        if m:
                            copy_turned(i * 4 + (m - 1))
                    copy_turned(i * 4 + 3)
                st.leave(NG // 4)

            def copy_turned(g):
                act.wait_ge(nat_ready, g + (NG + 2))
                act.sem_inc(carrier["act"], 1)
                for r in range(TPG):
                    st.mark(nc.scalar.activation(D[:, 7 * GROUP + r * P:7 * GROUP + (r + 1) * P],
                                                 psN[:, r * P:(r + 1) * P], ACT.Square,
                                                 accum_out=sm[:, 2, bass.ds(g * TPG + r, 1)]))
                st.settle(tell=sums_squared)
                nc.scalar.activation(tiles_of(AGG, g), psN[:, :], ACT.Copy).then_inc(nat_copied, 1)

            def chunk_tiles():
                for c in range(CHUNKS):
                    if c >= 2:
                        act.wait_ge(piece_multiplied[1], (c - 1) * NG * PPC + SLOTS)
                        act.wait_ge(h3_stored[c % 2], 16 * (c // 2))
                    with act.Fori(0, CT // 2) as i:
                        st.enter(i, 4)
                        for par in range(2):
                            t = i * 2 + (c * CT + par)
                            act.wait_ge(centered, t + 1)
                            act.sem_inc(carrier["act"], 1)
                            st.mark(nc.scalar.activation(psX[:, par * P:(par + 1) * P], xc[:, par, :], ACT.Square,
                                                         accum_out=tsc[:, par, 1:2]))
                            st.settle()
                            nc.scalar.activation(tsc[:, par, 2:3], tsc[:, par, 1:2], ACT.Sqrt, scale=1.0 / P,
                                                 bias=eps_col[:, :]).then_inc(rooted, 1)
                            act.wait_ge(scaled, t + 1)
                            act.sem_inc(carrier["act"], 1)
                            nc.scalar.activation(Hc[c % 2][:, bass.ds(i * 2 + par, 1), :],
                                                 xc[:, par, :].unsqueeze(1), ACT.Relu,
                                                 scale=tsc[:, par, 3:4]).then_inc(tiles_made, 1)
                            act.wait_ge(tiles_made, t + 3)
                            act.sem_inc(carrier["act"], 1)
                            st.mark(nc.scalar.activation(psY[:, 0:P].unsqueeze(1),
                                                         Hc[c % 2][:, bass.ds(i * 2 + par, 1), :], ACT.Square,
                                                         accum_out=R2[:, bass.ds(t, 1)]))
                            st.settle()
                    st.leave(CT // 2)
                    act.sem_inc(squared, 1)
                    act.wait_ge(tiles_made, (c + 1) * CT + 2)
                    nc.scalar.dma_start(h3[:, c * CT:(c + 1) * CT, :], Hc[c % 2])                      .then_inc(h3_stored[c % 2], 16)

            def artanh():
                job(sm[:, 13, :], sm[:, 12, :], ACT.Ln)

            def squares(A):
                for k in range(2):
                    job(SQ[:, HALF[k], :], A[:, HALF[k], :], ACT.Square)

            def layernorm():
                squares(H)
                job(sm[:, 1, :], sm[:, 0, :], ACT.Sqrt)

            act.sem_inc(piece_summed, SLOTS)
            act.sem_inc(pair_copied, 2)
            act.sem_inc(acc_copied, 1)
            act.sem_inc(nat_copied, 1)
            act.sem_inc(proj_out, 2)
            act.sem_inc(tiles_made, 2)
            act.wait_ge(weights_transposed, 1)
            st.mark(nc.scalar.activation(W[0][:, :], psX[:, 0:P], ACT.Copy))
            st.mark(nc.scalar.activation(W[2][:, :], psX[:, P:2 * P], ACT.Copy))
            st.settle()
            layernorm()
            project(0)
            adjacency_pass()
            job(sm[:, 3, :], sm[:, 3, :], ACT.Sqrt)
            layernorm()
            squares(H)
            project(1)
            squares(AGG)
            job(sm[:, 2:4, :], sm[:, 2:4, :], ACT.Sqrt)
            artanh()
            job(sm[:, 5, :], sm[:, 5, :], ACT.Tanh)
            turned_pass()
            job(sm[:, 2, :], sm[:, 2, :], ACT.Sqrt)
            artanh()
            job(sm[:, 4, :], sm[:, 4, :], ACT.Tanh, scale=0.5)
            artanh()
            job(sm[:, 6, :], sm[:, 6, :], ACT.Tanh)
            artanh()
            job(sm[:, 2, :], sm[:, 2, :], ACT.Sqrt)
            job(sm[:, 3, :], sm[:, 2, :], ACT.Tanh)
            layernorm()
            project(2)
            act.wait_ge(prefix_t, 1)
            nc.scalar.activation(pfx[:, 0, :], psX[:, 0:PREFIX], ACT.Copy).then_inc(prefix_copied, 1)
            act.wait_ge(prefix_n, 1)
            nc.scalar.activation(pfxn[:, :], psY[0:PREFIX, 0:P], ACT.Copy).then_inc(prefix_ready, 1)
            chunk_tiles()
            act.wait_ge(ring_done, 1)
            for par in range(2):
                act.wait_ge(h3_stored[par], 16 * CHUNKS // 2)
            nc.scalar.dma_start(SQ, h3).then_inc(h3_loaded, 16)
            for g in range(0, NG + 4, 2):
                if g < NG:
                    for k in (g, g + 1):
                        act.wait_ge(nat_ready, 2 * NG + k + 2)
                        nc.scalar.activation(AGG[:, k * TPG:(k + 1) * TPG, :], psN[:, :], ACT.Copy)\
                          .then_inc(nat_copied, 1)
                if g >= 4:
                    act.wait_ge(own_added, (g - 4) // 2 + 1)
                    for t in range((g - 4) * TPG, (g - 2) * TPG):
                        if t % TPG == 0:
                            st.settle()
                        st.mark(nc.scalar.activation(psY[:, (t % TPG) * P:(t % TPG + 1) * P], AGG[:, t, :],
                                                     ACT.Square, accum_out=sm[:, 0, t:t + 1]))
            st.settle(tell=sums_squared)
            job(sm[:, 2, :], sm[:, 2, :], ACT.Sqrt)
            artanh()
            job(sm[:, 4, :], sm[:, 4, :], ACT.Tanh, scale=0.5)
            artanh()
            project(3)
            job(sm[:, 2, :], sm[:, 2, :], ACT.Sqrt)
            job(sm[:, 3, :], sm[:, 2, :], ACT.Tanh)

        @block.vector
        def _(dve):
            v = nc.vector
            st = Steps(dve, dve_step, carrier["dve"])
            link, mark, settle = st.link, st.mark, st.settle
            asked = [0]

            def S(k):
                return sm[:, k, :]

            def ask():
                asked[0] += 1
                dve.sem_inc(for_act, 1)
                dve.wait_ge(from_act, asked[0])

            def by_row(a):
                return a.unsqueeze(2).to_broadcast([P, NT, P])

            def by_feature(n):
                return bias[:, n, :].unsqueeze(1).to_broadcast([P, NT, P])

            def layernorm():
                link(v.tensor_reduce(S(0), X[:, :, :], AX.X, ALU.add))
                link(v.tensor_scalar(S(0), S(0), -1.0 / P, None, ALU.mult))
                link(v.tensor_tensor(H[:, :, :], X[:, :, :], by_row(S(0)), ALU.add))
                squares(0)
                link(v.tensor_scalar(S(0), S(0), 1.0 / P, LN_EPS, ALU.mult, ALU.add))
                ask()
                link(v.reciprocal(S(1), S(1)))
                link(v.scalar_tensor_tensor(H[:, :, :], H[:, :, :], 0.0, by_row(S(1)), ALU.max, ALU.mult))

            def squares(k):
                dve.sem_inc(for_act, 2)
                for half in HALF:
                    asked[0] += 1
                    dve.wait_ge(from_act, asked[0])
                    mark(v.tensor_reduce(sm[:, k, half], SQ[:, half, :], AX.X, ALU.add))
                settle()

            def artanh(out, y):
                a, q, y2, m = S(12), S(11), S(10), S(9)
                link(v.tensor_scalar(q, y, -1.0, 1.0, ALU.mult, ALU.add))
                link(v.reciprocal(q, q))
                link(v.scalar_tensor_tensor(a, y, 1.0, q, ALU.add, ALU.mult))
                ask()
                link(v.tensor_tensor(y2, y, y, ALU.mult))
                link(v.tensor_scalar(q, y2, 1.0 / 13, None, ALU.mult))
                for k in (11, 9, 7, 5, 3):
                    link(v.scalar_tensor_tensor(q, q, 1.0 / k, y2, ALU.add, ALU.mult))
                link(v.scalar_tensor_tensor(q, q, 1.0, y, ALU.add, ALU.mult))
                link(v.tensor_scalar(m, y, 0.25, None, ALU.is_lt))
                link(v.scalar_tensor_tensor(q, S(13), -0.5, q, ALU.mult, ALU.add))
                link(v.tensor_tensor(q, q, m, ALU.mult))
                link(v.scalar_tensor_tensor(out, S(13), 0.5, q, ALU.mult, ALU.add))

            def project(n, src, dest, b=None):
                def stage(i, h):
                    dve.wait_ge(stage_read, i * 2 + (n * NG + h + 1))
                    dve.sem_inc(carrier["dve"], 1)
                    v.tensor_copy(AT[h][:, 0:GROUP], tiles_of(src, i * 2 + h)).then_inc(staged, 1)

                def take(i, h, g):
                    dve.wait_ge(projected, i * 2 + (n * NG + h + 1 + 2))
                    dve.sem_inc(carrier["dve"], 1)
                    ps = (psX, psY)[h][:, :].rearrange("p (r f) -> p r f", f=P)
                    if b is None:
                        v.tensor_copy(g, ps).then_inc(proj_out, 1)
                    else:
                        v.tensor_tensor(g, ps, bias[:, b, :].unsqueeze(1).to_broadcast([P, TPG, P]), ALU.add)\
                         .then_inc(proj_out, 1)

                for h in range(2):
                    stage(0, h)
                with dve.Fori(0, NG // 2 - 1) as i:
                    for h in range(2):
                        stage(i + 1, h)
                    for h in range(2):
                        take(i, h, tiles_of(dest, i * 2 + h))
                for h in range(2):
                    take(NG // 2 - 1, h, dest[:, (NG - 2 + h) * TPG:(NG - 1 + h) * TPG, :])
                dve.wait_ge(proj_out, (n + 1) * NG + 2)

            def pick(g):
                cf = [a.rearrange("p r c e -> p (r c e)") for a in (cand, cidx, cbase, pos)]
                kf = keys.rearrange("p r k -> p (r k)")
                pk.mark(v.tensor_tensor(kf, cf[1], cf[2], ALU.add))
                pk.mark(v.tensor_scalar(cf[3], cf[0], 0.0, None, ALU.is_gt))
                pk.mark(v.tensor_reduce(s4[:, 0, :], cand[:, :, :, 7], AX.X, ALU.max))
                pk.settle()
                pk.mark(v.tensor_tensor(kf, kf, cf[3], ALU.mult))
                pk.mark(v.tensor_reduce(s4[:, 1, :], pos.rearrange("p r c e -> p r (c e)"), AX.X, ALU.add))
                for r in range(TPG):
                    pk.mark(v.tensor_tensor_scan(zcum[:, r, :], ones, zero[:, r, :], 0.0, ALU.mult, ALU.add))
                pk.settle()
                pk.mark(v.tensor_scalar(s4[:, 2, :], s4[:, 1, :], -1.0, float(TOPK), ALU.mult, ALU.add))
                for rd in range(ROUNDS):
                    for r in range(TPG):
                        pk.mark(v.max(top[:, r, rd * 8:rd * 8 + 8], keys[:, r, :]))
                    pk.settle()
                    if rd + 1 < ROUNDS:
                        for r in range(TPG):
                            pk.mark(v.match_replace(keys[:, r, :], top[:, r, rd * 8:rd * 8 + 8], keys[:, r, :], 0.0))
                        pk.settle()
                pk.mark(v.tensor_tensor(zcum, zcum, s4[:, 2, :].unsqueeze(2).to_broadcast([P, TPG, PREFIX]), ALU.is_lt))
                pk.mark(v.tensor_scalar(topm, top, 0.0, None, ALU.is_gt))
                pk.mark(v.tensor_scalar(s4[:, 4, :], s4[:, 0, :], 0.0, None, ALU.is_gt))
                pk.settle()
                pk.mark(v.tensor_reduce(s4[:, 3, :], zcum, AX.X, ALU.add))
                pk.mark(v.scalar_tensor_tensor(s4[:, 4, :], s4[:, 1, :], float(TOPK) - 0.5, s4[:, 4, :], ALU.is_gt, ALU.max))
                pk.mark(v.tensor_scalar(s4[:, 5, :], s4[:, 6, :], 0.0, None, ALU.is_lt))
                pk.settle()
                pk.mark(v.tensor_scalar(s4[:, 3, :], s4[:, 3, :], float(N), None, ALU.add))
                pk.mark(v.tensor_tensor(tiles_of(FLAGS[:, 1, :], g), s4[:, 4, :], s4[:, 5, :], ALU.max))
                pk.mark(v.tensor_copy(tiles_of(FLAGS[:, 0, :], g), s4[:, 1, :]))
                pk.settle()
                slot0 = s4[:, 3, :].unsqueeze(2).to_broadcast([P, TPG, TOPK])
                pk.mark(v.scalar_tensor_tensor(topd, top, -1.0, slot0, ALU.add, ALU.subtract))
                pk.settle()
                pk.mark(v.tensor_tensor(topd, topd, topm, ALU.mult))
                pk.settle()
                pk.mark(v.tensor_tensor(tiles_of(IDX[:, :, 1:NGATHER], g), topd[:, :, 0:TOPK - 1],
                                        slot0[:, :, 0:TOPK - 1], ALU.add))
                pk.mark(v.tensor_copy(tiles_of(IDX[:, :, 0], g), s4[:, 3, :]))
                pk.settle()

            def scan_pass():
                with dve.Fori(0, NG) as g:
                    sc.enter(g, SCAN * NPC)
                    pk.enter(g, PICK)
                    for c in range(NPC):
                        dve.wait_ge(piece_loaded[c % SLOTS], g * (16 * K4) + 16 * (c // SLOTS + 1))
                        dve.sem_inc(carrier["dve"], 1)
                        pc = pieces[c % SLOTS]
                        if c == 0:
                            pk.mark(v.tensor_scalar(zero, pc[:, :, 0:PREFIX], 0.0, None, ALU.is_equal))
                            pk.mark(v.tensor_reduce(s4[:, 6, :], pc[:, :, 0:PREFIX], AX.X, ALU.min))
                            pk.settle()
                        found = []
                        for r in range(TPG + 1):
                            if r < TPG:
                                found.append(sc.mark(v.max(cand[:, r, c, :], pc[:, r, :])))
                            if r:
                                sc.settle(found[r - 1])
                                sc.mark(v.max_index(cidx[:, r - 1, c, :], cand[:, r - 1, c, :], pc[:, r - 1, :]))
                    sc.settle()
                    dve.wait_ge(pick_constants, 2)
                    pick(g)
                    dve.wait_ge(piece_summed, g * NPC + (NPC + SLOTS))
                    dve.sem_inc(carrier["dve"], 1)
                    pk.mark(v.tensor_reduce(tiles_of(RS[:, :], g), rs_part[:, :, :], AX.X, ALU.add))
                    pk.settle(tell=rs_reduced)
                sc.leave(NG)
                pk.leave(NG)

            def dot_pass():
                with dve.Fori(0, NG // 4) as i:
                    dt1.enter(i, 4 * sum(TAKES1))
                    st.enter(i, 12)
                    for m in range(4):
                        last = {}
                        for c in range(NPC):
                            dve.wait_ge(piece_loaded[c % SLOTS],
                                        i * (64 * K4) + 16 * ((NG + m) * K4 + c // SLOTS + 1))
                            dve.sem_inc(carrier["dve"], 1)
                            takes = [(b, dacc[:, b, :], dots) for b in range(BPP)]
                            if c % PPC == PPC - 1:
                                takes += [(b, dacc3[:, b - (BPP - EB), :], DINV) for b in range(BPP - EB, BPP)]
                            for k, (b, to, by) in enumerate(takes):
                                piece, scale = pieces_t[c % SLOTS][:, b, :], by[:, c * BPP + b:c * BPP + b + 1]
                                if k not in last:
                                    last[k] = dt1.mark(v.tensor_scalar(to, piece, scale, None, ALU.mult))
                                else:
                                    dt1.settle(last[k])
                                    last[k] = dt1.mark(v.scalar_tensor_tensor(to, piece, scale, to, ALU.mult, ALU.add))
                        dve.wait_ge(nat_ready, i * 4 + (m + NG))
                        dve.sem_inc(carrier["dve"], 1)
                        dt1.settle()
                        mark(v.tensor_tensor(dacc[:, 0:2, :], dacc[:, 0:2, :], dacc[:, 2:4, :], ALU.add))
                        mark(v.tensor_copy(dot1[1][m % 2], dacc3[:, 0, :]) if EB == 1 else
                             v.tensor_tensor(dot1[1][m % 2], dacc3[:, 0, :], dacc3[:, 1, :], ALU.add))
                        settle()
                        mark(v.tensor_tensor(dot1[0][m % 2], dacc[:, 0, :], dacc[:, 1, :], ALU.add))
                        settle(tell=dots_summed)
                dt1.leave(NG // 4)
                st.leave(NG // 4)
                dve.wait_ge(nat_copied, 2 * NG + 1)
                link(v.tensor_copy(DEN[:, :], psX[:, 0:NT]))
                link(v.tensor_copy(DEN3[:, :], psX[:, NT:2 * NT]))

            def general_form():
                STEPS = 3 * ROUNDS
                any_general = dve.value_load(CTL[0:1, 2, 0:1], min_val=0, max_val=1)
                with dve.If(any_general > 0):
                    ge = Steps(dve, general_step, carrier["dve"])
                    with dve.Fori(0, NT) as t:
                        general = dve.value_load(CTL[0:1, 1, bass.ds(t, 1)], min_val=0, max_val=1)
                        dve.wait_ge(row_loaded, t * 16 + 16)
                        dve.sem_inc(carrier["dve"], 1)
                        with dve.If(general > 0):
                            ge.enter(t, STEPS)
                            row = PIECES[:, 0:N]
                            for rd in range(ROUNDS):
                                ge.link(v.max(f8[:, :], row))
                                ge.link(v.max_index(fidx[:, rd * 8:rd * 8 + 8], f8[:, :], row))
                                if rd + 1 < ROUNDS:
                                    ge.link(v.match_replace(row, f8[:, :], row, -3.0e38))
                            ge.mark(v.tensor_copy(IDX[:, bass.ds(t, 1), :], fidx[:, :].unsqueeze(1)))
                            ge.settle(tell=row_used)
                        with dve.Else():
                            dve.sem_inc(general_step, STEPS)
                            dve.sem_inc(row_used, 1)
            def reduce_gathers(par, n, cuts):
                def reduce():
                    v.tensor_reduce(gmax[:, :], ring[par][:, 0:cuts[0], :].rearrange("p k f -> p f k"),
                                    AX.X, ALU.max).then_inc(gather_step, 1)
                if len(cuts) == 1:
                    reduce()
                    return
                with dve.If(n < cuts[0] + 1):
                    reduce()
                with dve.Else():
                    reduce_gathers(par, n, cuts[1:])

            def tile_maximum(c, i, par):
                n = dve.value_load(CTL[0:1, 0, bass.ds(i * 2 + (c * CT + par), 1)], min_val=1, max_val=NGATHER)
                dve.wait_ge(gathered[par], i * FULL + (c * CT // 2 + 1) * FULL)
                dve.sem_inc(carrier["dve"], 1)
                reduce_gathers(par, n, CUTS)
                gr.k += 1
                gr.settle()
                t = i * 2 + (c * CT + par)
                gr.mark(v.tensor_copy(idx_now[par][:, :], IDX[:, bass.ds(t + 2, 1), :]))
                gr.mark(v.tensor_tensor(X[:, bass.ds(t, 1), :], X[:, bass.ds(t, 1), :],
                                        gmax[:, :].unsqueeze(1), ALU.add))
                gr.settle(tell=idx_staged)

            def center_tile(c, i, par):
                t = i * 2 + (c * CT + par)
                gr.link(v.tensor_reduce(tsc[:, par, 0:1], X[:, bass.ds(t, 1), :], AX.X, ALU.add))
                gr.link(v.tensor_scalar(tsc[:, par, 0:1], tsc[:, par, 0:1], -1.0 / P, None, ALU.mult))
                dve.wait_ge(tiles_made, t + 1)
                dve.sem_inc(carrier["dve"], 1)
                gr.link(v.tensor_scalar(xc[:, par, :].unsqueeze(1), X[:, bass.ds(t, 1), :], tsc[:, par, 0:1], None,
                                        ALU.add), tell=centered)

            def scale_tile(c, i, par):
                t = i * 2 + (c * CT + par)
                dve.wait_ge(rooted, t + 1)
                dve.sem_inc(carrier["dve"], 1)
                gr.link(v.reciprocal(tsc[:, par, 3:4], tsc[:, par, 2:3]))
                gr.link(v.tensor_tensor(tsc[:, par, 3:4], tsc[:, par, 3:4], DINV[:, bass.ds(t, 1)], ALU.mult),
                        tell=scaled)

            def chunk_dots(c, i, pair):
                sums = {}
                for h in range(PPC):
                    for m in pair:
                        _, slot, loaded = chunk_piece(c, i, m, h)
                        dve.wait_ge(piece_loaded[slot], loaded)
                        dve.sem_inc(carrier["dve"], 1)
                    for b in range(TAKES3[h]):
                        j = c * CT + h * BPP + b
                        for m in pair:
                            slot = chunk_piece(c, i, m, h)[1]
                            so_far = DOT[:, bass.ds(i * GB + m, 1), :]
                            dt_.settle(sums.get(m, 0))
                            sums[m] = dt_.mark(v.scalar_tensor_tensor(so_far, pieces_t[slot][:, b:b + 1, :],
                                                                      DINV[:, j:j + 1], so_far, ALU.mult, ALU.add))

            def add_sums(c, i, m):
                g = i * GB + m
                n, _, _ = chunk_piece(c, i, m, PPC - 1)
                dve.wait_ge(piece_multiplied[1], n + (SLOTS + 1))
                dve.sem_inc(carrier["dve"], 1)
                so_far = ACC[:, bass.ds(g, 1), :]
                sa.mark(v.tensor_tensor(so_far, acc3[m % 4].unsqueeze(1), so_far, ALU.add))

            def add_own(g):
                dve.wait_ge(nat_copied, 2 * NG + g + 3)
                dve.wait_ge(h3_loaded, 16)
                two = slice(g * TPG, (g + 2) * TPG)
                link(v.tensor_tensor(AGG[:, two, :], AGG[:, two, :], SQ[:, two, :], ALU.add), tell=own_added)

            def add_expmap(least, tell=None):
                link(v.scalar_tensor_tensor(SQ, AGG[:, :, :], 0.0, AGG[:, :, :], ALU.max, ALU.mult))
                link(v.tensor_reduce(S(2), SQ, AX.X, ALU.add))
                link(v.tensor_scalar(S(2), S(2), least, None, ALU.max))
                ask()
                ask()
                link(v.reciprocal(S(2), S(2)))
                link(v.tensor_tensor(S(3), S(3), S(2), ALU.mult))
                for half in HALF:
                    link(v.scalar_tensor_tensor(AGG[:, half, :], AGG[:, half, :], 0.0, by_row(S(3))[:, half, :],
                                                ALU.max, ALU.mult))
                    link(v.tensor_tensor(X[:, half, :], X[:, half, :], AGG[:, half, :], ALU.add), tell=tell)

            sc = Steps(dve, piece_scanned[0], carrier["dve"])
            pk = Steps(dve, pick_step, carrier["dve"])
            dve.sem_inc(piece_scanned[0], SCAN * SLOTS)
            dve.sem_inc(rs_reduced, 1)
            dve.sem_inc(row_used, 1)
            link(v.memset(ones_col[:, :], 1.0))
            sc.base = SCAN * SLOTS
            dve.wait_ge(s_load, LOADS)
            dve.wait_ge(ident_ready, 2)
            link(v.tensor_scalar(alph[:, 1:2], alph[:, 0:1], -1.0, 1.0, ALU.mult, ALU.add))
            layernorm()
            project(0, H, H)
            dve.sem_inc(pass_ready, 1)
            scan_pass()
            dve.sem_inc(flags_ready, 1)
            dve.wait_ge(nat_copied, NG + 1)
            link(v.tensor_scalar(S(2), RS[:, :], alph[:, 0:1], alph[:, 1:2], ALU.mult, ALU.add))
            link(v.tensor_scalar(S(3), S(2), 0.0, None, ALU.is_equal))
            link(v.tensor_tensor(S(2), S(2), S(3), ALU.add))
            link(v.reciprocal(S(2), S(2)))
            link(v.tensor_scalar(S(3), S(3), -1.0, 1.0, ALU.mult, ALU.add))
            link(v.tensor_tensor(S(2), S(2), S(3), ALU.mult))
            link(v.scalar_tensor_tensor(AGG[:, :, :], H[:, :, :], alph[:, 1:2], AGG[:, :, :], ALU.mult, ALU.add))
            link(v.tensor_tensor(AGG[:, :, :], AGG[:, :, :], by_row(S(2)), ALU.mult))
            link(v.tensor_tensor(AGG[:, :, :], AGG[:, :, :], by_feature(0), ALU.add))
            link(v.scalar_tensor_tensor(X[:, :, :], AGG[:, :, :], 0.0, X[:, :, :], ALU.max, ALU.add))

            dve.wait_ge(flags_reduced, 1)
            link(v.tensor_scalar(ctlf[:, 1, :], FLAGR[0:1, 1, :], 0.0, None, ALU.is_gt))
            link(v.tensor_scalar(ctlf[:, 0, :], ctlf[:, 1, :], float(NGATHER), None, ALU.mult))
            link(v.scalar_tensor_tensor(ctlf[:, 0, :], FLAGR[0:1, 0, :], 1.0, ctlf[:, 0, :], ALU.add, ALU.max))
            link(v.tensor_scalar(CTL[:, 0, :], ctlf[:, 0, :], float(NGATHER), None, ALU.min))
            link(v.tensor_copy(CTL[:, 1, :], ctlf[:, 1, :]))
            link(v.tensor_reduce(CTL[:, 2, 0:1], ctlf[:, 1, :], AX.X, ALU.max), tell=ctl_ready)
            general_form()
            dve.sem_inc(piece_scanned[1], sum(TAKES1))
            dt1 = Steps(dve, piece_scanned[1], carrier["dve"])
            dt1.base = sum(TAKES1)
            link(v.tensor_scalar(S(3), RS[:, :], 1.0, None, ALU.add))
            ask()
            link(v.reciprocal(DINV[:, :], S(3)))

            layernorm()
            squares(2)
            dve.wait_ge(turned_stored, 1)
            project(1, H, AGG)
            squares(3)
            link(v.tensor_scalar(S(4), S(3), 0.0, None, ALU.add))
            link(v.tensor_scalar(sm[:, 2:4, :], sm[:, 2:4, :], 1e-30, None, ALU.max))
            ask()
            link(v.tensor_scalar(S(5), S(2), 1.0 - 1e-5, None, ALU.min))
            artanh(S(6), S(5))
            link(v.reciprocal(S(7), S(2)))
            link(v.tensor_tensor(S(5), S(3), S(7), ALU.mult))
            link(v.tensor_tensor(S(5), S(5), S(6), ALU.mult))
            ask()
            link(v.reciprocal(S(7), S(3)))
            link(v.tensor_tensor(S(7), S(7), S(5), ALU.mult))
            link(v.tensor_tensor(S(6), S(7), S(7), ALU.mult))
            link(v.tensor_tensor(S(6), S(6), S(4), ALU.mult))
            link(v.tensor_scalar(S(6), S(6), -1.0, 1.0, ALU.mult, ALU.add))
            link(v.tensor_scalar(S(6), S(6), 1e-5, None, ALU.max))
            link(v.reciprocal(S(6), S(6)))
            link(v.tensor_scalar(dots[:, :], S(6), 2.0, -1.0, ALU.mult, ALU.add))
            link(v.scalar_tensor_tensor(S(7), S(6), 2.0, S(7), ALU.mult, ALU.mult))
            link(v.tensor_tensor(H[:, :, :], AGG[:, :, :], by_row(S(7)), ALU.mult), tell=pass_ready)
            dot_pass()
            link(v.tensor_scalar(S(5), DEN[:, :], 1e-10, None, ALU.max))
            link(v.tensor_scalar(S(6), DEN[:, :], -1e-10, None, ALU.min))
            link(v.tensor_scalar(S(7), DEN[:, :], 0.0, None, ALU.is_ge))
            link(v.tensor_tensor(S(5), S(5), S(6), ALU.subtract))
            link(v.tensor_tensor(S(5), S(5), S(7), ALU.mult))
            link(v.tensor_tensor(S(5), S(5), S(6), ALU.add))
            link(v.reciprocal(S(8), S(5)))
            dve.wait_ge(sums_squared, NG)
            link(v.tensor_tensor(S(2), S(2), S(8), ALU.mult))
            link(v.tensor_tensor(S(2), S(2), S(8), ALU.mult))
            link(v.tensor_scalar(S(2), S(2), 1e-30, None, ALU.max))
            ask()
            link(v.tensor_scalar(S(3), S(2), 1.0 - 1e-5, None, ALU.min))
            artanh(S(4), S(3))
            ask()
            link(v.reciprocal(S(2), S(2)))
            link(v.tensor_tensor(S(8), S(8), S(2), ALU.mult))
            link(v.tensor_scalar(S(5), S(4), 1e-15, None, ALU.max))
            link(v.reciprocal(S(7), S(5)))
            link(v.tensor_tensor(S(4), S(4), S(7), ALU.mult))
            link(v.tensor_scalar(S(3), S(5), 1.0 - 1e-5, None, ALU.min))
            artanh(S(6), S(3))
            link(v.tensor_tensor(S(6), S(6), RS[:, :], ALU.mult))
            ask()
            link(v.tensor_tensor(S(6), S(6), S(4), ALU.mult))
            link(v.tensor_tensor(S(8), S(8), S(6), ALU.mult))
            link(v.tensor_scalar(S(5), S(6), -1.0, None, ALU.mult))
            link(v.tensor_tensor(S(5), S(5), S(6), ALU.max))
            link(v.tensor_scalar(S(5), S(5), 1e-15, None, ALU.max))
            link(v.tensor_scalar(S(3), S(5), 1.0 - 1e-5, None, ALU.min))
            artanh(S(4), S(3))
            link(v.reciprocal(S(5), S(5)))
            link(v.tensor_tensor(S(8), S(8), S(4), ALU.mult))
            link(v.tensor_tensor(S(8), S(8), S(5), ALU.mult))
            link(v.tensor_tensor(AGG[:, :, :], AGG[:, :, :], by_row(S(8)), ALU.mult))
            add_expmap(1e-30)

            layernorm()
            project(2, H, AGG, 1)
            dve.wait_ge(prefix_copied, 1)
            link(v.tensor_tensor_scan(pfx[:, 1, :], pfx[:, 0, :], pfx[:, 0, :], -3.0e38, ALU.max, ALU.max),
                 tell=prefix_scanned)
            gr = Steps(dve, gather_step, carrier["dve"])
            dt_ = Steps(dve, piece_scanned[2], carrier["dve"])
            dve.sem_inc(piece_scanned[2], sum(TAKES3))
            dt_.base = sum(TAKES3)
            sa = Steps(dve, sums_added, carrier["dve"])
            dve.sem_inc(sums_added, 4)
            sa.base = 4
            for par in range(2):
                gr.link(v.tensor_copy(idx_now[par][:, :], IDX[:, par, :]), tell=idx_staged)
            mark(v.memset(H[:, :, :], 0.0))
            mark(v.memset(eps_col[:, :], LN_EPS))
            dve.wait_ge(table_stored, STORES)
            mark(v.memset(AGG[:, :, :], 0.0))
            settle()
            for c in range(CHUNKS):
                with dve.Fori(0, CT // 2) as i:
                    dense = c > 0
                    gr.enter(i, 16)
                    if dense:
                        dt_.enter(i, sum(TAKES3))
                        sa.enter(i, GB)
                    for m in range(0, GB, 2):
                        par, half = divmod(m, GB // 2)
                        if half == 0:
                            tile_maximum(c, i, par)
                        if dense:
                            chunk_dots(c - 1, i, (m, m + 1))
                        if half == 0:
                            center_tile(c, i, par)
                        if dense and m:
                            add_sums(c - 1, i, m - 2)
                            add_sums(c - 1, i, m - 1)
                        if half == GB // 2 - 2:
                            scale_tile(c, i, par)
                    if dense:
                        add_sums(c - 1, i, GB - 2)
                        add_sums(c - 1, i, GB - 1)
                gr.leave(CT // 2)
                if dense:
                    dt_.leave(CT // 2)
                    sa.leave(CT // 2)
            dve.sem_inc(ring_done, 1)
            dt_.enter(0, CT // 2 * sum(TAKES3))
            sa.enter(0, NG)
            for g in range(0, NG, 2):
                chunk_dots(CHUNKS - 1, g // GB, (g % GB, g % GB + 1))
                dt_.settle()
                for k in (g, g + 1):
                    add_sums(CHUNKS - 1, k // GB, k % GB)
                if g >= 4:
                    add_own(g - 4)
            dt_.leave(1)
            sa.leave(1)
            add_own(NG - 4)
            add_own(NG - 2)
            mark(v.tensor_tensor(DEN[:, :], psX[:, 0:NT], DEN3[:, :], ALU.add))
            settle()
            dve.wait_ge(squared, CHUNKS)
            link(v.tensor_scalar(S(3), RS[:, :], 1.0, None, ALU.add))
            link(v.tensor_tensor(S(2), R2[:, :], S(3), ALU.mult))
            link(v.tensor_scalar(S(2), S(2), -1.0, 1.0, ALU.mult, ALU.add))
            link(v.reciprocal(S(2), S(2)))
            link(v.tensor_scalar(S(7), S(2), 2.0, 1e7, ALU.mult, ALU.min))
            link(v.tensor_tensor(S(5), DEN[:, :], DINV[:, :], ALU.add))
            link(v.scalar_tensor_tensor(S(5), S(7), -1.0, S(5), ALU.add, ALU.mult))
            link(v.reciprocal(S(5), S(5)))
            link(v.tensor_tensor(S(5), S(5), S(7), ALU.mult))
            dve.wait_ge(sums_squared, NG + 1)
            link(v.tensor_tensor(S(2), S(0), S(5), ALU.mult))
            link(v.tensor_tensor(S(2), S(2), S(5), ALU.mult))
            link(v.tensor_scalar(S(2), S(2), 1e-30, None, ALU.max))
            ask()
            link(v.tensor_scalar(S(3), S(2), 1e-7, 1.0 - 1e-7, ALU.max, ALU.min))
            artanh(S(4), S(3))
            ask()
            link(v.reciprocal(S(6), S(3)))
            link(v.tensor_tensor(S(8), S(4), S(6), ALU.mult))
            link(v.tensor_tensor(S(3), S(2), S(8), ALU.mult))
            link(v.tensor_tensor(S(8), S(8), S(5), ALU.mult))
            link(v.tensor_scalar(S(3), S(3), 1e-7, 1.0 - 1e-7, ALU.max, ALU.min))
            artanh(S(4), S(3))
            link(v.reciprocal(S(3), S(3)))
            link(v.tensor_tensor(S(8), S(8), S(4), ALU.mult))
            link(v.tensor_tensor(S(8), S(8), S(3), ALU.mult))
            link(v.tensor_tensor(H[:, :, :], AGG[:, :, :], by_row(S(8)), ALU.mult))
            project(3, H, AGG, 2)
            add_expmap(1e-14, tell=x_done)


_INS = ["x", "adj", "L0_gnn_alpha", "L0_gnn_W", "L0_gnn_b", "L1_gnn_W", "L2_gnn_W", "L2_gnn_b", "L3_gnn_W",
        "L3_gnn_b"]


def kernel(**inputs):
    import numpy as np
    import concourse.bacc as bacc
    from concourse.bass_utils import run_bass_kernel_spmd

    nc = bacc.Bacc("TRN2", target_bir_lowering=False, num_devices=1)
    arrays, args = {}, []
    for name in _INS:
        a = np.ascontiguousarray(inputs[name])
        arrays[f"in_{name}"] = a
        args.append(nc.dram_tensor(f"in_{name}", a.shape, mybir.dt.from_np(a.dtype), kind="ExternalInput").ap())
    out = nc.dram_tensor("out_x", inputs["x"].shape, mybir.dt.float32, kind="ExternalOutput").ap()
    build(nc, *args, out)
    r = run_bass_kernel_spmd(nc, [arrays], core_ids=[0])
    return r.results[0]["out_x"]
```
